# Optimizing a Trainium2 kernel written in Bass

```python
import numpy as np
import jax
import jax.numpy as jnp

def _softmax(x, axis=-1):
    return jax.nn.softmax(x, axis=axis)

def _gelu(x):
    return jax.nn.gelu(x, approximate=True)

def _silu(x):
    return jax.nn.silu(x)

def _sigmoid(x):
    return jax.nn.sigmoid(x)

def _layernorm(x, axis=-1, eps=1e-05):
    m = jnp.mean(x, axis=axis, keepdims=True)
    v = jnp.var(x, axis=axis, keepdims=True)
    return (x - m) / jnp.sqrt(v + eps)

def _scatter_add(tgt, idx, src, axis=0):
    return tgt.at[idx].add(src)

def _segment_sum(src, seg, n):
    return jax.ops.segment_sum(src, seg, n)
kernel_name = 'mk_seq_postln_d1_jaxref_r4_a9acad'

def setup_inputs(seed: int=0):
    np.random.seed(seed)
    _w = jnp.asarray

    def _L0_attn_setup():
        import jax, jax.numpy as jnp
        import numpy as np
        D_MODEL = 256
        N_HEADS = 16
        HEAD_DIM = D_MODEL // N_HEADS
        BUCKET = 64
        key = jax.random.key(seed)
        k1, k2, k3 = jax.random.split(key, 3)
        B, T = (4, 1024)
        x = jax.random.normal(k1, (B, T, D_MODEL), dtype=jnp.float32)
        W_qkv = jax.random.normal(k2, (3 * D_MODEL, D_MODEL), dtype=jnp.float32) * D_MODEL ** (-0.5)
        W_out = jax.random.normal(k3, (D_MODEL, D_MODEL), dtype=jnp.float32) * D_MODEL ** (-0.5)
        return {'x': x, 'W_qkv': W_qkv, 'W_out': W_out}
    _L0_attn_in = _L0_attn_setup()

    def _L0_ffn_setup():
        import jax, jax.numpy as jnp
        import numpy as np
        D_MODEL = 256
        D_FF = 1024
        N_EXPERTS = 8
        TOP_K = 2

        def _ffn(x, w1, b1, w2, b2):
            h = jax.nn.gelu(x @ w1.T + b1)
            return h @ w2.T + b2
        key = jax.random.key(seed)
        ks = jax.random.split(key, 12)
        s = 0.02
        x = jax.random.normal(ks[0], (4, 512, D_MODEL), dtype=jnp.float32)
        shared_w1 = jax.random.normal(ks[1], (D_FF, D_MODEL), dtype=jnp.float32) * s
        shared_b1 = jnp.zeros((D_FF,), dtype=jnp.float32)
        shared_w2 = jax.random.normal(ks[2], (D_MODEL, D_FF), dtype=jnp.float32) * s
        shared_b2 = jnp.zeros((D_MODEL,), dtype=jnp.float32)
        router_w = jax.random.normal(ks[3], (N_EXPERTS, D_MODEL), dtype=jnp.float32) * s
        router_b = jnp.zeros((N_EXPERTS,), dtype=jnp.float32)
        spec_w1 = jax.random.normal(ks[4], (N_EXPERTS, D_FF, D_MODEL), dtype=jnp.float32) * s
        spec_b1 = jnp.zeros((N_EXPERTS, D_FF), dtype=jnp.float32)
        spec_w2 = jax.random.normal(ks[5], (N_EXPERTS, D_MODEL, D_FF), dtype=jnp.float32) * s
        spec_b2 = jnp.zeros((N_EXPERTS, D_MODEL), dtype=jnp.float32)
        return dict(x=x, shared_w1=shared_w1, shared_b1=shared_b1, shared_w2=shared_w2, shared_b2=shared_b2, router_w=router_w, router_b=router_b, spec_w1=spec_w1, spec_b1=spec_b1, spec_w2=spec_w2, spec_b2=spec_b2)
    _L0_ffn_in = _L0_ffn_setup()
    _d = {'L0_attn_x': _L0_attn_in['x'], 'L0_attn_W_qkv': _L0_attn_in['W_qkv'], 'L0_attn_W_out': _L0_attn_in['W_out'], 'L0_ffn_shared_w1': _L0_ffn_in['shared_w1'], 'L0_ffn_shared_b1': _L0_ffn_in['shared_b1'], 'L0_ffn_shared_w2': _L0_ffn_in['shared_w2'], 'L0_ffn_shared_b2': _L0_ffn_in['shared_b2'], 'L0_ffn_router_w': _L0_ffn_in['router_w'], 'L0_ffn_router_b': _L0_ffn_in['router_b'], 'L0_ffn_spec_w1': _L0_ffn_in['spec_w1'], 'L0_ffn_spec_b1': _L0_ffn_in['spec_b1'], 'L0_ffn_spec_w2': _L0_ffn_in['spec_w2'], 'L0_ffn_spec_b2': _L0_ffn_in['spec_b2']}
    _x0 = _d['L0_attn_x']
    _d['L0_attn_x'] = jax.random.normal(jax.random.fold_in(jax.random.key(seed), 1), (4, 1024, 256), dtype=_x0.dtype)
    del _x0
    return _d

def reference(L0_attn_x, L0_attn_W_qkv, L0_attn_W_out, L0_ffn_shared_w1, L0_ffn_shared_b1, L0_ffn_shared_w2, L0_ffn_shared_b2, L0_ffn_router_w, L0_ffn_router_b, L0_ffn_spec_w1, L0_ffn_spec_b1, L0_ffn_spec_w2, L0_ffn_spec_b2):

    def _L0_attn_ref(x, W_qkv, W_out):
        import jax, jax.numpy as jnp
        import numpy as np
        D_MODEL = 256
        N_HEADS = 16
        HEAD_DIM = D_MODEL // N_HEADS
        BUCKET = 64
        B, T, _ = x.shape
        qkv = x @ W_qkv.T
        qkv = qkv.reshape(B, T, 3 * N_HEADS, HEAD_DIM).transpose(0, 2, 1, 3)
        q, k, v = jnp.split(qkv, 3, axis=1)
        q = jax.nn.softmax(q, axis=-1) * HEAD_DIM ** (-0.5)
        k = jnp.exp(k)
        n = T // BUCKET
        bucket = lambda t: t.reshape(B, N_HEADS, n, BUCKET, HEAD_DIM)
        b_q, b_k, b_v = (bucket(q), bucket(k), bucket(v))
        b_k_sum = jnp.sum(b_k, axis=-2)
        b_k_cumsum = jnp.cumsum(b_k_sum, axis=-2)
        b_k_cumsum = jnp.pad(b_k_cumsum, ((0, 0), (0, 0), (1, 0), (0, 0)))[:, :, :-1]
        context = jnp.einsum('bhnsd,bhnse->bhnde', b_k, b_v)
        context = jnp.cumsum(context, axis=-3)
        context = jnp.pad(context, ((0, 0), (0, 0), (1, 0), (0, 0), (0, 0)))[:, :, :-1]
        den = jnp.einsum('bhnsd,bhnd->bhns', b_q, b_k_cumsum)
        D_inv = 1.0 / jnp.maximum(den, 1e-06)
        attn = jnp.einsum('bhnsd,bhnde,bhns->bhnse', b_q, context, D_inv)
        xo = attn.reshape(B, N_HEADS, T, HEAD_DIM)
        xo = xo.transpose(0, 2, 1, 3).reshape(B, T, D_MODEL)
        return xo @ W_out.T

    def _L0_ffn_ref(x, shared_w1, shared_b1, shared_w2, shared_b2, router_w, router_b, spec_w1, spec_b1, spec_w2, spec_b2):
        import jax, jax.numpy as jnp
        import numpy as np
        D_MODEL = 256
        D_FF = 1024
        N_EXPERTS = 8
        TOP_K = 2

        def _ffn(x, w1, b1, w2, b2):
            h = jax.nn.gelu(x @ w1.T + b1)
            return h @ w2.T + b2
        B, T, D = x.shape
        xf = x.reshape(-1, D)
        U = xf.shape[0]
        logits = xf @ router_w.T + router_b
        routing = jax.nn.softmax(logits, axis=-1)
        sel_w, sel_idx = jax.lax.top_k(routing, TOP_K)
        sel_w = sel_w / sel_w.sum(axis=-1, keepdims=True)
        comb = jnp.zeros_like(routing).at[jnp.arange(U)[:, None], sel_idx].set(sel_w)
        shared_out = _ffn(xf, shared_w1, shared_b1, shared_w2, shared_b2)

        def body(acc, params):
            w1, b1, w2, b2, we = params
            return (acc + we[:, None] * _ffn(xf, w1, b1, w2, b2), None)
        acc0 = jnp.zeros_like(shared_out)
        acc, _ = jax.lax.scan(body, acc0, (spec_w1, spec_b1, spec_w2, spec_b2, comb.T))
        return (shared_out + acc).reshape(B, T, D)
    x = L0_attn_x
    x = _layernorm(x + _L0_attn_ref(x, L0_attn_W_qkv, L0_attn_W_out), axis=-1)
    x = _layernorm(x + _L0_ffn_ref(x, L0_ffn_shared_w1, L0_ffn_shared_b1, L0_ffn_shared_w2, L0_ffn_shared_b2, L0_ffn_router_w, L0_ffn_router_b, L0_ffn_spec_w1, L0_ffn_spec_b1, L0_ffn_spec_w2, L0_ffn_spec_b2), axis=-1)
    return x

_drawn_inputs = setup_inputs


def setup_inputs(seed=0):
    import zlib

    import numpy as np

    out = dict(_drawn_inputs(seed))
    spreads = {'L0_ffn_shared_b1': (0.0, 0.1),
     'L0_ffn_shared_b2': (0.0, 0.1),
     'L0_ffn_router_b': (0.0, 0.1),
     'L0_ffn_spec_b1': (0.0, 0.324),
     'L0_ffn_spec_b2': (0.0, 0.1)}
    factors = {}
    for name, (base, spread) in spreads.items():
        noise = np.random.default_rng([zlib.crc32(name.encode()), seed]).standard_normal(out[name].shape)
        drawn = base * np.exp(spread * noise) if base else spread * noise
        out[name] = jnp.asarray(drawn.astype(out[name].dtype))
    for name, factor in factors.items():
        out[name] = (out[name] * factor).astype(out[name].dtype)
    return out
```

```python
from contextlib import ExitStack, contextmanager

import concourse.bass as bass
from concourse import mybir

F32 = mybir.dt.float32
I32 = mybir.dt.int32
HALF = mybir.dt.bfloat16
ALU = mybir.AluOpType
ACT = mybir.ActivationFunctionType
X = mybir.AxisListType.X

P = 128
B, T, D = 4, 1024, 256
N_TOK = B * T
HEADS, HD = 16, 16
BUCKET = 64
FF = 1024
EXPERTS = 8
TOP = 2
KC = D // P
FC = FF // P
TILES = N_TOK // P
BT = T // P
GH = P // HD
CW = P + GH
NW = CW + GH
TILE = 2 * P
SLOT_TILES = TOP * N_TOK // TILE + EXPERTS - 1
SLOTS = SLOT_TILES * TILE
HALF_SHARED = N_TOK // TILE // 2
N_FFN = 2 * HALF_SHARED + SLOT_TILES
TAIL = HALF_SHARED + SLOT_TILES
EW = 2 * KC * FF
CHUNK = 1024
W_CHUNKS = (EXPERTS + 1) * EW // CHUNK
NEG = -0.5
EPS = 1e-5
LN_LAG = 2

C_ID = 0
C_MASK = C_ID + P
C_TRI = C_MASK + CW
C_ONE = C_TRI + P
C_REV = C_ONE + P
C_SEG = C_REV + EXPERTS
C_THR = C_SEG + EXPERTS * TILES
C_J = C_THR + TILES // 2
C_NEG = C_J + N_FFN
C_RB = C_NEG + 1
C_N = C_RB + EXPERTS


def build(nc, xT_d, x_d, wqkv_d, wout_d, ffn_d, b1_d, b2_d, rw_d, const_d, out_d):
    with ExitStack() as ctx:
        def sb(name, shape, dt):
            return ctx.enter_context(nc.sbuf_tensor(name, shape, dt))

        def sem(name):
            return ctx.enter_context(nc.semaphore(name))

        def sems(name, n):
            return [sem(f"{name}{i}") for i in range(n)]

        x2_d = nc.dram_tensor("x2_rows", (N_TOK, D), F32, kind="Internal").ap()
        tok_d = nc.dram_tensor("token_rows_split", (N_TOK, 2 * D), HALF, kind="Internal").ap()
        slot_d = nc.dram_tensor("slot_rows_split", (SLOTS, 2 * D), HALF, kind="Internal").ap()
        ytok_d = nc.dram_tensor("shared_out_rows", (N_TOK, D), F32, kind="Internal").ap()
        yslot_d = nc.dram_tensor("slot_out_rows", (SLOTS, D), F32, kind="Internal").ap()

        W = sb("weights", [P, (EXPERTS + 1) * 2 * EW], HALF)
        const = sb("const", [P, C_N], F32)
        ident_h = sb("ident_h", [P, P], HALF)
        b1 = sb("b1", [P, (EXPERTS + 1) * FC], F32)
        rw = sb("rw", [P, KC, EXPERTS], F32)
        zero = sb("zero", [P, SLOTS * 2 * D // (TILES * P)], HALF)
        logits = sb("logits", [P, TILES, EXPERTS], F32)
        gate = sb("gate", [P, TOP, TILES], F32)
        slot_f = sb("slot_f", [P, TILES, TOP], F32)
        slot_i = sb("slot_i", [P, TILES, TOP], I32)
        small = sb("small", [P, 16 * TILES], F32)
        expert_f = sb("expert_f", [P, N_FFN], F32)
        expert_i = sb("expert_i", [P, N_FFN], I32)
        ident = const[:, C_ID:C_ID + P]
        mask = const[:, C_MASK:C_MASK + CW]

        region = sb("region", [P, 12200], F32)
        at = {"A": 0, "B": 0}

        def carve(stage, cols, dt=F32):
            n = cols if dt is not HALF else cols // 2
            v = region[:, at[stage]:at[stage] + n]
            at[stage] += n
            assert at[stage] <= 12200, at
            return v if dt is F32 else v.bitcast(dt)

        xT = [carve("A", KC * TILE).rearrange("p (c n) -> p c n", c=KC) for _ in range(2)]
        xr = [carve("A", D) for _ in range(4)]
        stage = [carve("A", CHUNK) for _ in range(2)]
        wqkv = carve("A", KC * 3 * D).rearrange("p (c n) -> p c n", c=KC)
        wout = carve("A", KC * D).rearrange("p (c n) -> p c n", c=KC)
        qs = carve("A", D)
        eq = [carve("A", D) for _ in range(2)]
        ek = [carve("A", D) for _ in range(2)]
        vx = [carve("A", KC * CW).rearrange("p (g n) -> p g n", g=KC) for _ in range(2)]
        qT = [carve("A", D) for _ in range(2)]
        mc = [carve("A", KC * NW).rearrange("p (g n) -> p g n", g=KC) for _ in range(2)]
        attn = [carve("A", D) for _ in range(2)]
        attnT = [carve("A", D) for _ in range(2)]
        s = carve("A", D)
        x2 = [carve("A", D) for _ in range(2)]
        x2s = [carve("A", 2 * D, HALF) for _ in range(2)]
        x2T = carve("A", D)
        qmax = carve("A", HEADS)
        den = carve("A", HEADS)
        rden = carve("A", HEADS)
        stats = carve("A", 6)
        mv = [carve("A", 2) for _ in range(2)]
        ve = carve("A", 1)
        rstd = [carve("A", 1) for _ in range(2)]

        rows = [carve("B", 2 * 2 * D, HALF).rearrange("p (h n) -> p h n", h=2) for _ in range(2)]
        XT = [carve("B", 4 * TILE, HALF).rearrange("p (k h n) -> p k h n", k=4, h=2) for _ in range(2)]
        hf = [carve("B", 2 * TILE) for _ in range(2)]
        hh = carve("B", FC * TILE, HALF).rearrange("p (f n) -> p f n", f=FC)
        hl = carve("B", FC * TILE, HALF).rearrange("p (f n) -> p f n", f=FC)
        yo = [carve("B", 2 * D).rearrange("p (h n) -> p h n", h=2) for _ in range(2)]
        b2 = [carve("B", D) for _ in range(2)]
        sc_at = at["B"]
        ring = [[carve("B", D) for _ in range(4)] for _ in range(4)]
        cstats = carve("B", 6)
        cmv = [carve("B", 2) for _ in range(4)]
        cve = carve("B", 1)
        crstd = [carve("B", 1) for _ in range(4)]
        idx = [carve("B", 8).bitcast(I32) for _ in range(2)]
        sc = [region[:, sc_at + i * 4 * D:sc_at + (i + 1) * 4 * D].bitcast(HALF)
              .rearrange("p (t n) -> p t n", t=4) for i in range(2)]
        n_te = TILES * EXPERTS
        r_tmp = [region[:, i * n_te:(i + 1) * n_te] for i in range(8)]

        bank = [ctx.enter_context(nc.psum_tensor(f"bank{i}", [P, 512], F32)) for i in range(8)]
        Q, KV, EQT, CTX, NUM, ATT, WO, X2B = bank
        ctx_ps = CTX[:, 0:KC * CW].rearrange("p (g n) -> p g n", g=KC)
        num_ps = NUM[:, 0:KC * NW].rearrange("p (g n) -> p g n", g=KC)
        H = bank[0:4]
        Y = bank[4:6]
        TB = [b[:, :].bitcast(HALF)[:, 0:4 * P] for b in bank[6:8]]
        PRE, TOT = bank[4], bank[5]

        s_const, s_w0 = sem("s_const"), sem("s_w0")
        s_init, s_passed = sem("s_init"), sem("s_passed")
        ld_xT, ld_xr, ld_w = sems("ld_xT", 2), sems("ld_xr", 4), sems("ld_w", 2)
        st_x2, st_rows, st_zero = sems("st_x2", 2), sems("st_rows", 2), sem("st_zero")
        s_q, s_kv, s_eqT, s_ctx = sem("s_q"), sem("s_kv"), sem("s_eqT"), sem("s_ctx")
        s_num, s_attnT, s_wo = sem("s_num"), sem("s_attnT"), sem("s_wo")
        s_x2T, s_lg = sem("s_x2T"), sem("s_lg")
        s_qmax, s_qsub, s_mask, s_den, s_attn = sem("s_qmax"), sem("s_qsub"), sem("s_mask"), sem("s_den"), sem("s_attn")
        s_res, s_st, s_mv, s_x2, s_lgo = sem("s_res"), sem("s_st"), sem("s_mv"), sem("s_x2"), sem("s_lgo")
        s_expk, s_vc, s_expq, s_qTe = sem("s_expk"), sem("s_vc"), sem("s_expq"), sem("s_qTe")
        s_aTe, s_x2Te = sem("s_aTe"), sem("s_x2Te")
        s_ws, s_ve, s_rstd, s_split = sem("s_ws"), sem("s_ve"), sem("s_rstd"), sem("s_split")
        s_r, s_rexp, s_rsub, s_hot, s_rank, s_slots, s_experts = (
            sem("s_r"), sem("s_rexp"), sem("s_rsub"), sem("s_hot"), sem("s_rank"), sem("s_slots"), sem("s_experts"))
        ld_rows, ld_b2, st_y = sems("ld_rows", 2), sems("ld_b2", 2), sems("st_y", 2)
        ld_sc, st_sc, ld_c, ld_g, st_out = sems("ld_sc", 2), sems("st_sc", 2), sems("ld_c", 4), sems("ld_g", 4), sems("st_out", 4)
        s_T, s_h, s_y = sem("s_T"), sem("s_h"), sem("s_y")
        s_XT, s_g = sem("s_XT"), sem("s_g")
        s_hi, s_lo, s_yo = sem("s_hi"), sem("s_lo"), sem("s_yo")
        s_idx, s_cadd, s_cmv, s_cfin, s_cve, s_crstd = sem("s_idx"), sem("s_cadd"), sem("s_cmv"), sem("s_cfin"), sem("s_cve"), sem("s_crstd")

        block = ctx.enter_context(nc.Block())

        def wait(eng, semaphore, n, alone=False):
            if not isinstance(n, int) or n > 0:
                eng.wait_ge(semaphore, n)
            if not isinstance(n, int) and (alone or eng.engine == mybir.EngineType.Pool):
                eng.sem_inc(s_passed, 1)

        def live(t, lag, n=TILES):
            return not isinstance(t, int) or 0 <= t - lag < n

        @contextmanager
        def loop(eng, start, end, by):
            with eng.Fori(0, (end - start) // by) as n:
                yield n * by + start

        def steps_A(eng, step):
            for t in range(BT):
                step(t, t)
            with loop(eng, BT, TILES, BT) as t0:
                for k in range(BT):
                    step(t0 + k, k)
            for t in range(TILES, TILES + 3):
                step(t, t % BT)

        def half_of(k):
            return (k // 2) % 2

        def loads(t, k, per, more):
            return (t - k) * (16 // per) + (k // per + more) * 16

        @block.sync
        def _(sp):
            sp.dma_start(const[:], const_d).then_inc(s_const, 16)
            sp.dma_start(wqkv, wqkv_d).then_inc(s_w0, 16)
            sp.dma_start(xT[0], xT_d[:, :, 0:TILE]).then_inc(ld_xT[0], 16)
            sp.dma_start(wout, wout_d).then_inc(s_w0, 16)
            sp.dma_start(rw[:], rw_d).then_inc(s_w0, 16)
            sp.dma_start(b1[:], b1_d).then_inc(s_w0, 16)
            sp.dma_start(stage[0], ffn_d[0]).then_inc(ld_w[0], 16)
            zero_v = slot_d.rearrange("(t p r) n -> t p (r n)", t=TILES, p=P) if SLOTS % (TILES * P) == 0 else \
                slot_d.rearrange("s n -> (s n)").rearrange("(t p m) -> t p m", t=TILES, p=P)
            tok_v = tok_d.rearrange("(t p) n -> t p n", p=P)
            x2_v = x2_d.rearrange("(t p) n -> t p n", p=P)
            x_v = x_d.rearrange("(t p) n -> t p n", p=P)

            def one(view, i):
                return view[i] if isinstance(i, int) else view[bass.ds(i, 1)].rearrange("a p n -> p (a n)")

            def step(t, k):
                if live(t, 0):
                    if k == 0 and isinstance(t, int):
                        sp.wait_ge(s_init, 1)
                    sp.dma_start(one(zero_v, t), zero[:]).then_inc(st_zero, 16)
                    wait(sp, s_res, t - 3)
                    sp.dma_start(xr[k % 4], one(x_v, t)).then_inc(ld_xr[k % 4], 16)
                if k % 2 == 0 and live(t, -2):
                    wait(sp, s_kv, t, alone=True)
                    src = xT_d[:, :, (t + 2) * P:(t + 4) * P] if isinstance(t, int) else \
                        xT_d[:, :, bass.ds((t + 2) * P, TILE)]
                    if isinstance(t, int) or k < BT - 2:
                        sp.dma_start(xT[half_of(k + 2)], src).then_inc(ld_xT[half_of(k + 2)], 16)
                if live(t, -1, W_CHUNKS):
                    wait(sp, s_ws, 2 * t)
                    sp.dma_start(stage[(k + 1) % 2], one(ffn_d, t + 1)).then_inc(ld_w[(k + 1) % 2], 16)
                if live(t, 3):
                    wait(sp, s_x2, t - 2)
                    sp.dma_start(one(x2_v, t - 3), x2[(k + 1) % 2]).then_inc(st_x2[(k + 1) % 2], 16)
                    wait(sp, s_split, 2 * (t - 2))
                    sp.dma_start(one(tok_v, t - 3), x2s[(k + 1) % 2]).then_inc(st_rows[(k + 1) % 2], 16)

            for t in range(BT):
                step(t, t)
            with loop(sp, BT, TILES - BT, BT) as t0:
                for k in range(BT):
                    step(t0 + k, k)
                sp.dma_start(xT[0], xT_d[:, :, bass.ds((t0 + BT) * P, TILE)]).then_inc(ld_xT[0], 16)
            for t in range(TILES - BT, TILES + 3):
                step(t, t % BT)

            sp.wait_ge(s_lgo, TILES)
            sp.wait_ge(s_ws, 2 * W_CHUNKS)
            for i in range(2):
                sp.wait_ge(st_x2[i], 16 * TILES // 2)
                sp.wait_ge(st_rows[i], 16 * TILES // 2)
            sp.wait_ge(s_slots, 1)
            ffn_tok = tok_d.rearrange("(t h p) n -> t p h n", h=2, p=P)
            ffn_slot = slot_d.rearrange("(t h p) n -> t p h n", h=2, p=P)
            y_tok = ytok_d.rearrange("(t h p) n -> t p h n", h=2, p=P)
            y_slot = yslot_d.rearrange("(t h p) n -> t p h n", h=2, p=P)

            def of(view, i):
                return view[i] if isinstance(i, int) else view[bass.ds(i, 1)].rearrange("a p h n -> p (a h) n")

            def load_rows(i, p, view, j):
                wait(sp, s_T, 2 * (i - 1))
                sp.dma_start(rows[p], of(view, j)).then_inc(ld_rows[p], 16)

            def load_b2(i, p):
                e = sp.value_load(expert_i[0:1, i:i + 1] if isinstance(i, int) else expert_i[0:1, bass.ds(i, 1)],
                                  min_val=0, max_val=EXPERTS)
                wait(sp, s_yo, 2 * (i - 1))
                sp.dma_start(b2[p], b2_d[bass.ds(e, 1), :].rearrange("a n -> (a n)").partition_broadcast(P))\
                    .then_inc(ld_b2[p], 16)

            def store_y(i, p, view, j):
                wait(sp, s_yo, 2 * (i + 1))
                sp.dma_start(of(view, j), yo[p]).then_inc(st_y[p], 16)

            def combine_io(c, q):
                if live(c, 4):
                    wait(sp, s_cfin, c - 3)
                    sp.dma_start(one(out_v, c - 4), ring[q][3]).then_inc(st_out[q], 16)
                if live(c, 0):
                    sp.dma_start(ring[q][0], one(x2_v, c)).then_inc(ld_c[q], 16)
                    sp.dma_start(ring[q][1], one(yt_v, c)).then_inc(ld_c[q], 16)

            out_v = out_d.rearrange("(t p) n -> t p n", p=P)
            yt_v = ytok_d.rearrange("(t p) n -> t p n", p=P)

            for i in range(2):
                load_rows(i, i, ffn_tok, i)
                load_b2(i, i)
            h2 = HALF_SHARED - 2
            with loop(sp, 0, h2, 2) as i0:
                for p in range(2):
                    i = i0 + p
                    load_rows(i + 2, p, ffn_tok, i + 2)
                    store_y(i, p, y_tok, i)
                    load_b2(i + 2, p)
            for i in range(h2, HALF_SHARED):
                p = i % 2
                if i == h2:
                    for q in range(2):
                        sp.wait_ge(st_sc[q], 16 * TOP * TILES // 2)
                load_rows(i + 2, p, ffn_slot, i - h2)
                store_y(i, p, y_tok, i)
                load_b2(i + 2, p)
            h = HALF_SHARED
            pairs = (SLOT_TILES - 2) // 2 * 2
            with loop(sp, h, h + pairs, 2) as i0:
                for p in range(2):
                    i = i0 + p
                    load_rows(i + 2, p, ffn_slot, i + 2 - h)
                    store_y(i, p, y_slot, i - h)
                    load_b2(i + 2, p)
            for i in range(h + pairs, TAIL):
                p = i % 2
                if i + 2 < TAIL:
                    load_rows(i + 2, p, ffn_slot, i + 2 - h)
                else:
                    load_rows(i + 2, p, ffn_tok, i + 2 - SLOT_TILES)
                store_y(i, p, y_slot, i - h)
                load_b2(i + 2, p)

            def tail(i, c0, p):
                last = isinstance(i, int) and i + 2 >= N_FFN
                if not last:
                    load_rows(i + 2, p, ffn_tok, i + 2 - SLOT_TILES)
                if isinstance(i, int):
                    sp.wait_ge(st_y[1 - p], 16 * (i // 2 if p else (i + 1) // 2))
                else:
                    sp.wait_ge(st_y[1 - p], 8 * (i - p) + (16 if p else 0))
                for q in range(4):
                    if not (isinstance(i, int) and i == N_FFN - 1 and q >= 2):
                        combine_io(c0 + q, q)
                store_y(i, p, y_tok, i - SLOT_TILES)
                if not last:
                    load_b2(i + 2, p)

            tail(TAIL, 0, TAIL % 2)
            tail(TAIL + 1, 4, (TAIL + 1) % 2)
            with loop(sp, TAIL + 2, TAIL + 6, 2) as i0:
                for j in range(2):
                    tail(i0 + j, (i0 + (j - TAIL)) * 4, (TAIL + j) % 2)
            tail(N_FFN - 2, TILES - 8, (N_FFN - 2) % 2)
            tail(N_FFN - 1, TILES - 4, (N_FFN - 1) % 2)
            sp.wait_ge(st_y[(N_FFN - 1) % 2], 16 * ((N_FFN + 1) // 2))
            for c in range(TILES - 2, TILES + 4):
                combine_io(c, c % 4)
            for q in range(4):
                sp.wait_ge(st_out[q], 16 * TILES // 4)
            sp.wait_ge(st_y[0], 16 * ((N_FFN + 1) // 2))
            sp.wait_ge(st_y[1], 16 * (N_FFN // 2))
            sp.wait_ge(st_zero, 16 * TILES)

        @block.tensor
        def _(pe):
            pe.wait_ge(s_const, 16)
            pe.wait_ge(s_w0, 64)
            pe.wait_ge(s_init, 2)

            def context(u, k, r):
                n = 2 * u + r
                wait(pe, s_mask, n + 1)
                if r == 0:
                    wait(pe, s_expk, u + 1)
                    wait(pe, s_vc, u + 1)
                rows_ = slice(BUCKET * r, BUCKET * (r + 1))
                for g in range(KC):
                    mm = pe.matmul(ctx_ps[:, g, :], ek[k % 2][rows_, g * P:(g + 1) * P], vx[k % 2][rows_, g, :],
                                   start=(k == 0 and r == 0 and g == 0), stop=(k == BT - 1 and r == 1),
                                   skip_group_check=True)
                mm.then_inc(s_ctx, 1)

            def step(t, k):
                if live(t, 1):
                    context(t - 1, (k - 1) % BT, 0)
                    wait(pe, s_expq, t)
                    wait(pe, s_qTe, t - 1)
                    for g in range(KC):
                        mm = pe.transpose(EQT[:, g * P:(g + 1) * P], eq[(k - 1) % 2][:, g * P:(g + 1) * P], ident)
                    mm.then_inc(s_eqT, 1)
                if live(t, 2):
                    wait(pe, s_attn, t - 1)
                    wait(pe, s_aTe, t - 2)
                    for g in range(KC):
                        mm = pe.transpose(ATT[:, g * P:(g + 1) * P], attn[k % 2][:, g * P:(g + 1) * P], ident)
                    mm.then_inc(s_attnT, 1)
                if live(t, 3):
                    wait(pe, s_x2, t - 2)
                    wait(pe, s_lgo, t - 3)
                    for g in range(KC):
                        mm = pe.transpose(X2B[:, g * P:(g + 1) * P], x2[(k + 1) % 2][:, g * P:(g + 1) * P], ident)
                    mm.then_inc(s_x2T, 1)
                if live(t, 0):
                    wait(pe, ld_xT[half_of(k)], loads(t, k, 4, 1))
                    xt = xT[half_of(k)]
                    cols = slice((k % 2) * P, (k % 2 + 1) * P)
                    wait(pe, s_qsub, t)
                    for c in range(KC):
                        mm = pe.matmul(Q[:, 0:D], xt[:, c, cols], wqkv[:, c, 0:D], start=(c == 0), stop=(c == KC - 1))
                    mm.then_inc(s_q, 1)
                    wait(pe, s_vc, t)
                    for c in range(KC):
                        mm = pe.matmul(KV[:, :], xt[:, c, cols], wqkv[:, c, D:3 * D], start=(c == 0), stop=(c == KC - 1))
                    mm.then_inc(s_kv, 1)
                if live(t, 1):
                    wait(pe, s_qTe, t)
                    wait(pe, s_attn, t - 1)
                    for r in range(2):
                        wait(pe, s_mask, 2 * (t - 1) + r + 1)
                        for g in range(KC):
                            o = g * P + BUCKET * r
                            mm = pe.matmul(num_ps[BUCKET * r:BUCKET * (r + 1), g, :],
                                           qT[(k - 1) % 2][:, o:o + BUCKET], mc[r][:, g, :], start=True, stop=True)
                    mm.then_inc(s_num, 1)
                    context(t - 1, (k - 1) % BT, 1)
                if live(t, 2):
                    wait(pe, s_aTe, t - 1)
                    wait(pe, s_res, t - 2)
                    for g in range(KC):
                        mm = pe.matmul(WO[:, 0:D], attnT[k % 2][:, g * P:(g + 1) * P], wout[:, g, :],
                                       start=(g == 0), stop=(g == KC - 1))
                    mm.then_inc(s_wo, 1)
                if live(t, 3):
                    wait(pe, s_x2Te, t - 2)
                    for g in range(KC):
                        mm = pe.matmul(X2B[:, D:D + EXPERTS], x2T[:, g * P:(g + 1) * P], rw[:, g, :],
                                       start=(g == 0), stop=(g == KC - 1))
                    mm.then_inc(s_lg, 1)

            steps_A(pe, step)

            pe.wait_ge(s_hot, 1)
            pe.matmul(PRE[:, 0:n_te], const[:, C_TRI:C_TRI + P], r_tmp[0], start=True, stop=True).then_inc(s_rank, 1)
            pe.matmul(TOT[:, 0:n_te], const[:, C_ONE:C_ONE + P], r_tmp[0], start=True, stop=True).then_inc(s_rank, 1)

            def turn(i, p):
                wait(pe, s_XT, 2 * i)
                wait(pe, ld_rows[p], 8 * (i - p) + 16)
                for h in range(2):
                    for k in range(4):
                        mm = pe.transpose(TB[h][:, k * P:(k + 1) * P], rows[p][:, h, k * P:(k + 1) * P], ident_h[:])
                    mm.then_inc(s_T, 1)

            def tile(i, p, more=True):
                e = pe.value_load(expert_i[0:1, i:i + 1] if isinstance(i, int) else expert_i[0:1, bass.ds(i, 1)],
                                  min_val=0, max_val=EXPERTS)
                base = pe.snap(e * (2 * EW))
                wait(pe, s_XT, 2 * i + 2)
                for f in range(FC):
                    wait(pe, s_g, 8 * i + f - 3)
                    terms = [(part, c, xpart) for part, xpart in ((0, 0), (0, 1), (1, 0)) for c in range(KC)]
                    for n, (part, c, xpart) in enumerate(terms):
                        o = part * EW + c * FF + f * P
                        mm = pe.matmul(H[f % 4][:, 0:TILE], W[:, bass.ds(base + o, P)],
                                       XT[p][:, xpart * KC + c].rearrange("p h n -> p (h n)"),
                                       start=(n == 0), stop=(n == len(terms) - 1))
                    mm.then_inc(s_h, 1)
                if more:
                    turn(i + 1, 1 - p)
                wait(pe, s_yo, 2 * i)
                for f in range(FC):
                    if f % 2 == 0:
                        wait(pe, s_lo, 4 * i + f // 2 + 1)
                    for part, src in ((0, hh), (1, hh), (0, hl)):
                        w2 = W[:, bass.ds(base + (part * EW + KC * FF + f * D), D)]
                        for h in range(2):
                            mm = pe.matmul(Y[h][:, 0:D], src[:, f, h * P:(h + 1) * P], w2,
                                           start=(f == 0 and part == 0 and src is hh),
                                           stop=(f == FC - 1 and src is hl))
                mm.then_inc(s_y, 1)

            pe.wait_ge(s_experts, 1)
            pe.wait_ge(s_slots, 1)
            pe.wait_ge(s_ws, 2 * W_CHUNKS)
            turn(0, 0)
            tile(0, 0)
            with loop(pe, 1, N_FFN - 2, 2) as i0:
                for j in range(2):
                    tile(i0 + j, (1 + j) % 2)
            for i in range((N_FFN - 2) // 2 * 2 + 1, N_FFN):
                tile(i, i % 2, i + 1 < N_FFN)

        @block.scalar
        def _(act):
            act.wait_ge(s_init, 2)

            def step(t, k):
                if live(t, 1):
                    wait(act, s_eqT, t)
                    wait(act, s_num, t - 2)
                    act.activation(qT[(k - 1) % 2], EQT[:, 0:D], ACT.Copy).then_inc(s_qTe, 1)
                if live(t, 2):
                    wait(act, s_attnT, t - 1)
                    wait(act, s_wo, t - 3)
                    act.activation(attnT[k % 2], ATT[:, 0:D], ACT.Copy).then_inc(s_aTe, 1)
                if live(t, 3):
                    wait(act, s_x2T, t - 2)
                    wait(act, s_lg, t - 3)
                    act.activation(x2T, X2B[:, 0:D], ACT.Copy).then_inc(s_x2Te, 1)
                if live(t, 0):
                    wait(act, s_qsub, t + 1)
                    wait(act, s_eqT, t - 1)
                    act.activation(eq[k % 2], qs, ACT.Exp).then_inc(s_expq, 1)
                    wait(act, s_kv, t + 1)
                    wait(act, s_ctx, 2 * (t - 1))
                    act.activation(ek[k % 2], KV[:, 0:D], ACT.Exp).then_inc(s_expk, 1)
                    act.activation(vx[k % 2][:, :, 0:P], KV[:, D:2 * D].rearrange("p (g n) -> p g n", g=KC),
                                   ACT.Copy).then_inc(s_vc, 1)

            steps_A(act, step)

            act.wait_ge(s_rsub, 1)
            act.activation(r_tmp[1], r_tmp[0], ACT.Exp).then_inc(s_rexp, 1)

            def evacuate(i, p):
                for h in range(2):
                    wait(act, s_T, 2 * i + h + 1)
                    act.activation(XT[p][:, :, h, :], TB[h].rearrange("p (k n) -> p k n", k=4), ACT.Copy)\
                        .then_inc(s_XT, 1)

            def tile(i, p, more=True):
                e = act.value_load(expert_i[0:1, i:i + 1] if isinstance(i, int) else expert_i[0:1, bass.ds(i, 1)],
                                   min_val=0, max_val=EXPERTS)
                for f in range(FC):
                    wait(act, s_h, 8 * i + f + 1)
                    if f % 2 == 0:
                        wait(act, s_lo, 4 * i + f // 2 - 1)
                    act.activation(hf[f // 2 % 2][:, f % 2 * TILE:(f % 2 + 1) * TILE], H[f % 4][:, 0:TILE],
                                   ACT.Gelu_apprx_tanh, bias=b1[:, bass.ds(e * FC + f, 1)]).then_inc(s_g, 1)
                if more:
                    evacuate(i + 1, 1 - p)

            act.wait_ge(s_experts, 1)
            evacuate(0, 0)
            tile(0, 0)
            with loop(act, 1, N_FFN - 2, 2) as i0:
                for j in range(2):
                    tile(i0 + j, (1 + j) % 2)
            for i in range((N_FFN - 2) // 2 * 2 + 1, N_FFN):
                tile(i, i % 2, i + 1 < N_FFN)

        @block.vector
        def _(dve):
            dve.memset(zero[:], 0.0).then_inc(s_init, 1)
            for j in range(2):
                dve.memset(vx[j][:, :, P:CW], 1.0)
            dve.wait_ge(s_const, 16)
            for j in range(2):
                for g in range(KC):
                    dve.tensor_copy(mc[j][:, g, CW:NW], mask[:, P:CW])
            dve.tensor_copy(ident_h[:], ident).then_inc(s_init, 1)

            def context_before(n, k, r):
                if k == 0 and r == 0:
                    dve.memset(mc[0][:, :, 0:CW], 0.0).then_inc(s_mask, 1)
                else:
                    dve.tensor_tensor(mc[r][:, :, 0:CW], ctx_ps, mask.unsqueeze(1).to_broadcast([P, KC, CW]),
                                      ALU.mult).then_inc(s_mask, 1)

            def heads(ap):
                return ap.rearrange("p (h d) -> p h d", d=HD)

            def over_heads(ap):
                return ap.unsqueeze(2).to_broadcast([P, HEADS, HD])

            def step(t, k):
                if live(t, 1):
                    wait(dve, s_ctx, 2 * (t - 1) + 1)
                    wait(dve, s_num, t - 1)
                    context_before(2 * (t - 1) + 1, (k - 1) % BT, 1)
                if live(t, 0):
                    wait(dve, s_q, t + 1)
                    dve.tensor_reduce(qmax, heads(Q[:, 0:D]), X, ALU.max).then_inc(s_qmax, 1)
                    wait(dve, s_qmax, t + 1)
                    wait(dve, s_expq, t)
                    dve.tensor_tensor(heads(qs), heads(Q[:, 0:D]), over_heads(qmax), ALU.subtract)\
                        .then_inc(s_qsub, 1)
                if live(t, 1):
                    wait(dve, s_num, t)
                    sums = num_ps[:, :, CW:NW]
                    dve.tensor_scalar(rden.rearrange("p (g h) -> p g h", g=KC), sums, 4e-6, None, ALU.mult)\
                        .then_inc(s_den, 1)
                    wait(dve, s_den, 3 * (t - 1) + 1)
                    dve.tensor_tensor(den.rearrange("p (g h) -> p g h", g=KC), num_ps[:, :, P:CW],
                                      rden.rearrange("p (g h) -> p g h", g=KC), ALU.max).then_inc(s_den, 1)
                    wait(dve, s_den, 3 * (t - 1) + 2)
                    dve.reciprocal(rden, den).then_inc(s_den, 1)
                    wait(dve, s_den, 3 * (t - 1) + 3)
                    wait(dve, s_attnT, t - 2)
                    dve.tensor_tensor(attn[(k - 1) % 2].rearrange("p (g h d) -> p g h d", g=KC, d=HD),
                                      num_ps[:, :, 0:P].rearrange("p g (h d) -> p g h d", d=HD),
                                      rden.rearrange("p (g h) -> p g h", g=KC).unsqueeze(3)
                                      .to_broadcast([P, KC, GH, HD]), ALU.mult).then_inc(s_attn, 1)
                if live(t, 0):
                    wait(dve, s_ctx, 2 * t)
                    wait(dve, s_num, t)
                    context_before(2 * t, k, 0)
                if live(t, 2):
                    wait(dve, s_wo, t - 1)
                    wait(dve, ld_xr[(k - 2) % 4], loads(t, k, 4, 1 if k % 4 >= 2 else 0))
                    dve.tensor_tensor(s, WO[:, 0:D], xr[(k - 2) % 4], ALU.add).then_inc(s_res, 1)
                    wait(dve, s_res, t - 1)
                    dve.bn_stats(stats, s).then_inc(s_st, 1)
                    wait(dve, s_st, t - 1)
                    wait(dve, s_rstd, t - 3, alone=True)
                    dve.bn_aggr(mv[k % 2], stats).then_inc(s_mv, 1)
                if live(t, 3):
                    wait(dve, s_lg, t - 2)
                    row = logits[:, t - 3, :] if isinstance(t, int) else \
                        logits[:, bass.ds(t - 3, 1), :].rearrange("p a e -> p (a e)")
                    dve.tensor_tensor(row, X2B[:, D:D + EXPERTS], const[:, C_RB:C_RB + EXPERTS], ALU.add)\
                        .then_inc(s_lgo, 1)
                if live(t, 2):
                    wait(dve, s_mv, t - 1)
                    wait(dve, s_rstd, t - 1)
                    wait(dve, st_x2[k % 2], loads(t, k, 2, -1))
                    wait(dve, s_split, 2 * (t - 3))
                    wait(dve, s_x2T, t - 3)
                    dve.tensor_scalar(x2[k % 2], s, mv[k % 2][:, 0:1], rstd[k % 2], ALU.subtract, ALU.mult)\
                        .then_inc(s_x2, 1)

            steps_A(dve, step)

            done = [0]

            def then(ins, also=None):
                done[0] += 1
                ins.then_inc(s_r, 1)
                dve.wait_ge(s_r, done[0])

            def te(ap):
                return ap.rearrange("p (t e) -> p t e", e=EXPERTS)

            def over_e(ap):
                return ap.unsqueeze(2).to_broadcast([P, TILES, EXPERTS])

            col = [small[:, i * TILES:(i + 1) * TILES] for i in range(16)]
            top1, top2, first, inv, summed = col[0:5]
            rev = const[:, C_REV:C_REV + EXPERTS].unsqueeze(1).to_broadcast([P, TILES, EXPERTS])
            dve.wait_ge(s_lgo, TILES)
            L = logits[:]
            prob, hot1, hot2, tmp = r_tmp[1], r_tmp[2], r_tmp[3], r_tmp[4]
            then(dve.tensor_reduce(top1, L, X, ALU.max))
            dve.tensor_tensor(te(r_tmp[0]), L, over_e(top1), ALU.subtract).then_inc(s_rsub, 1)
            dve.wait_ge(s_rexp, 1)
            then(dve.tensor_reduce(summed, te(prob), X, ALU.add))
            then(dve.reciprocal(inv, summed))
            then(dve.tensor_tensor(te(prob), te(prob), over_e(inv), ALU.mult))
            for top, hot in ((top1, hot1), (top2, hot2)):
                then(dve.tensor_reduce(top, te(prob), X, ALU.max))
                then(dve.tensor_tensor(te(tmp), te(prob), over_e(top), ALU.is_equal))
                then(dve.tensor_tensor(te(tmp), te(tmp), rev, ALU.mult))
                then(dve.tensor_reduce(first, te(tmp), X, ALU.max))
                then(dve.tensor_tensor(te(hot), rev, over_e(first), ALU.is_equal))
                if hot is hot1:
                    then(dve.scalar_tensor_tensor(prob, hot, -2.0, prob, ALU.mult, ALU.add))
            dve.tensor_tensor(r_tmp[0], hot1, hot2, ALU.add).then_inc(s_hot, 1)
            then(dve.tensor_tensor(summed, top1, top2, ALU.add))
            then(dve.reciprocal(inv, summed))
            dve.tensor_tensor(gate[:, 0, :], top1, inv, ALU.mult)
            then(dve.tensor_tensor(gate[:, 1, :], top2, inv, ALU.mult))
            tot, upto, excl = r_tmp[5], r_tmp[6], r_tmp[7]

            def et(ap):
                return ap.rearrange("p (e t) -> p e t", t=TILES)

            dve.wait_ge(s_rank, 2)
            then(dve.tensor_copy(et(tot), TOT[:, 0:n_te].rearrange("p (t e) -> p e t", e=EXPERTS)))
            then(dve.tensor_tensor_scan(upto, const[:, C_SEG:C_SEG + n_te], tot, 0.0, ALU.mult, ALU.add))
            then(dve.tensor_tensor(excl, upto, tot, ALU.subtract))
            nthr = TILES // 2
            over = tot[:, 0:EXPERTS * nthr]
            counts = et(upto)[:, :, TILES - 1]
            then(dve.tensor_tensor(over.rearrange("p (e j) -> p e j", j=nthr),
                                   counts.unsqueeze(2).to_broadcast([P, EXPERTS, nthr]),
                                   const[:, C_THR:C_THR + nthr].unsqueeze(1).to_broadcast([P, EXPERTS, nthr]),
                                   ALU.is_gt))
            n_e, end_e, base_e = col[5][:, 0:EXPERTS], col[6][:, 0:EXPERTS], col[7][:, 0:EXPERTS]
            then(dve.tensor_reduce(n_e, over.rearrange("p (e j) -> p e j", j=nthr), X, ALU.add))
            then(dve.tensor_tensor_scan(end_e, const[:, C_ONE:C_ONE + EXPERTS], n_e, 0.0, ALU.mult, ALU.add))
            then(dve.tensor_tensor(base_e, end_e, n_e, ALU.subtract))
            then(dve.tensor_scalar(base_e, base_e, float(TILE), None, ALU.mult))
            then(dve.tensor_tensor(et(excl), et(excl), base_e.unsqueeze(2).to_broadcast([P, EXPERTS, TILES]), ALU.add))
            then(dve.tensor_tensor(te(tmp), PRE[:, 0:n_te].rearrange("p (t e) -> p t e", e=EXPERTS),
                                   excl.rearrange("p (e t) -> p t e", t=TILES), ALU.add))
            for j, hot in enumerate((hot1, hot2)):
                then(dve.tensor_tensor(hot, hot, tmp, ALU.mult))
                then(dve.tensor_reduce(slot_f[:, :, j], te(hot), X, ALU.add))
            then(dve.tensor_copy(slot_i[:].rearrange("p t j -> p (t j)"), slot_f[:].rearrange("p t j -> p (t j)")))
            ej = r_tmp[5:7]
            for h0 in (0, 1):
                lo, hi = (0, 28) if h0 == 0 else (28, N_FFN)
                n = hi - lo
                a = ej[h0][:, 0:n * EXPERTS].rearrange("p (j e) -> p j e", e=EXPERTS)
                then(dve.tensor_tensor(a, end_e.unsqueeze(1).to_broadcast([P, n, EXPERTS]),
                                       const[:, C_J + lo:C_J + hi].unsqueeze(2).to_broadcast([P, n, EXPERTS]),
                                       ALU.is_le))
                then(dve.tensor_reduce(expert_f[:, lo:hi], a, X, ALU.add))
            then(dve.tensor_scalar(expert_f[:], expert_f[:], float(EXPERTS - 1), None, ALU.min))
            dve.memset(expert_f[:, 0:HALF_SHARED], float(EXPERTS))
            then(dve.memset(expert_f[:, TAIL:N_FFN], float(EXPERTS)))
            dve.tensor_copy(expert_i[:], expert_f[:]).then_inc(s_experts, 1)
            dve.wait_ge(s_experts, 1)
            dve.engine_nop().then_inc(s_slots, 1)

            def split(i, g):
                wait(dve, s_g, 8 * i + 2 * g + 2)
                if g == 0:
                    wait(dve, s_y, i)
                src = hf[g % 2]
                dve.tensor_copy(hh[:, 2 * g:2 * g + 2].rearrange("p f n -> p (f n)"), src).then_inc(s_hi, 1)
                wait(dve, s_hi, 4 * i + g + 1)
                dve.tensor_tensor(hl[:, 2 * g:2 * g + 2].rearrange("p f n -> p (f n)"), src,
                                  hh[:, 2 * g:2 * g + 2].rearrange("p f n -> p (f n)"), ALU.subtract)\
                    .then_inc(s_lo, 1)

            def outputs(i, p):
                wait(dve, s_y, i + 1)
                wait(dve, ld_b2[p], 8 * (i - p) + 16)
                wait(dve, st_y[p], 8 * (i - p))
                for h in range(2):
                    dve.tensor_tensor(yo[p][:, h, :], Y[h][:, 0:D], b2[p], ALU.add).then_inc(s_yo, 1)

            def gate_of(j, c):
                return gate[:, j, c:c + 1] if isinstance(c, int) else gate[:, j, bass.ds(c, 1)]

            def combine(c, q):
                if live(c, 0):
                    r = ring[q]
                    wait(dve, ld_c[q], 8 * (c - q) + 32)
                    wait(dve, ld_g[q], 8 * (c - q) + 32)
                    dve.tensor_tensor(r[0], r[0], r[1], ALU.add).then_inc(s_cadd, 1)
                    wait(dve, s_cadd, 4 * c + 1)
                    dve.scalar_tensor_tensor(r[0], r[2], gate_of(0, c), r[0], ALU.mult, ALU.add).then_inc(s_cadd, 1)
                    wait(dve, s_cadd, 4 * c + 2)
                    dve.scalar_tensor_tensor(r[2], r[3], gate_of(1, c), r[0], ALU.mult, ALU.add).then_inc(s_cadd, 1)
                    wait(dve, s_cadd, 4 * c + 3)
                    dve.bn_stats(cstats, r[2]).then_inc(s_cadd, 1)
                    wait(dve, s_cadd, 4 * c + 4, alone=True)
                    dve.bn_aggr(cmv[q], cstats).then_inc(s_cmv, 1)
                if live(c, LN_LAG):
                    o = (q - LN_LAG) % 4
                    wait(dve, s_crstd, c - LN_LAG + 1)
                    dve.tensor_scalar(ring[o][3], ring[o][2], cmv[o][:, 0:1], crstd[o], ALU.subtract, ALU.mult)\
                        .then_inc(s_cfin, 1)

            def tile(i, p, c0=None, qs_=range(4)):
                for g in range(4):
                    split(i, g)
                    if c0 is not None and g in qs_:
                        combine(c0 + g, g)
                outputs(i, p)

            tile(0, 0)
            tile(1, 1)
            with loop(dve, 2, TAIL - 1, 2) as i0:
                for p in range(2):
                    tile(i0 + p, p)
            tile(TAIL - 1, (TAIL - 1) % 2)
            tile(TAIL, TAIL % 2, 0)
            tile(TAIL + 1, (TAIL + 1) % 2, 4)
            with loop(dve, TAIL + 2, TAIL + 6, 2) as i0:
                for j in range(2):
                    tile(i0 + j, (TAIL + j) % 2, (i0 + (j - TAIL)) * 4)
            tile(N_FFN - 2, (N_FFN - 2) % 2, TILES - 8)
            tile(N_FFN - 1, (N_FFN - 1) % 2, TILES - 4, range(2))
            for c in range(TILES - 2, TILES + LN_LAG):
                combine(c, c % 4)

        @block.gpsimd
        def _(pool):
            pool.wait_ge(s_const, 16)
            neg = const[:, C_NEG:C_NEG + 1]

            def split_weights(t, k):
                o = t // 4 * (2 * EW) + t % 4 * CHUNK if isinstance(t, int) else \
                    (t - k) * (2 * EW // 4) + (k // 4 * (2 * EW) + k % 4 * CHUNK)
                def part(n):
                    b_ = o + n * EW
                    return W[:, b_:b_ + CHUNK] if isinstance(t, int) else W[:, bass.ds(b_, CHUNK)]
                wait(pool, ld_w[k % 2], loads(t, k, 2, 1))
                pool.tensor_copy(part(0), stage[k % 2]).then_inc(s_ws, 1)
                wait(pool, s_ws, 2 * t + 1)
                pool.tensor_tensor(part(1), stage[k % 2], part(0), ALU.subtract).then_inc(s_ws, 1)

            def step(t, k):
                if live(t, 2):
                    wait(pool, s_mv, t - 1)
                    pool.tensor_scalar(ve, mv[k % 2][:, 1:2], EPS, None, ALU.add).then_inc(s_ve, 1)
                    wait(pool, s_ve, t - 1)
                    wait(pool, s_x2, t - 3)
                    pool.tensor_tensor(rstd[k % 2], ve, neg, ALU.pow).then_inc(s_rstd, 1)
                    wait(pool, s_x2, t - 1)
                    wait(pool, st_rows[k % 2], loads(t, k, 2, -1))
                    pool.tensor_copy(x2s[k % 2][:, 0:D], x2[k % 2]).then_inc(s_split, 1)
                    wait(pool, s_split, 2 * (t - 2) + 1)
                    pool.tensor_tensor(x2s[k % 2][:, D:2 * D], x2[k % 2], x2s[k % 2][:, 0:D], ALU.subtract)\
                        .then_inc(s_split, 1)
                split_weights(t, k)

            steps_A(pool, step)
            split_weights(W_CHUNKS - 1, (W_CHUNKS - 1) % BT)

            pool.wait_ge(s_slots, 1)
            pool.wait_ge(st_zero, 16 * TILES)
            for i in range(2):
                pool.wait_ge(st_rows[i], 16 * TILES // 2)
                pool.wait_ge(st_x2[i], 16 * TILES // 2)
            sc_v = tok_d.rearrange("(g t p) n -> g p t n", t=4, p=P)

            def copy_index(n, g, j):
                src = slot_i[:, 4 * g:4 * g + 4, :] if isinstance(g, int) else slot_i[:, bass.ds(g * 4, 4), :]
                pool.tensor_copy(idx[j], src.rearrange("p t j -> p (t j)")).then_inc(s_idx, 1)
                wait(pool, s_idx, n)

            def load_sc(g, j):
                wait(pool, st_sc[j], 64 * (g - j))
                src = sc_v[g] if isinstance(g, int) else sc_v[bass.ds(g, 1)].rearrange("a p t n -> p (a t) n")
                pool.dma_start(sc[j], src).then_inc(ld_sc[j], 16)

            def scatter(g, j):
                wait(pool, ld_sc[j], 8 * (g - j) + 16)
                copy_index(g + 1, g, j)
                for t in range(4):
                    for k in range(TOP):
                        pool.indirect_dma_start(slot_d, bass.IndirectOffsetOnAxis(ap=idx[j][:, 2 * t + k:2 * t + k + 1], axis=0),
                                                sc[j][:, t, :], None).then_inc(st_sc[j], 16)

            groups = TILES // 4
            for g in range(2):
                load_sc(g, g)
            scatter(0, 0)
            scatter(1, 1)
            with loop(pool, 2, groups, 2) as g0:
                for j in range(2):
                    load_sc(g0 + j, j)
                for j in range(2):
                    scatter(g0 + j, j)

            for p in range(2):
                n = (TAIL + 1 - p) // 2
                pool.wait_ge(st_y[p], 16 * n)
                pool.wait_ge(st_sc[p], 16 * TOP * TILES // 2)

            def gather(c, q, j):
                if live(c, 0):
                    wait(pool, s_cfin, c - 3)
                    wait(pool, st_out[q], 4 * (c - q))
                    for k in range(TOP):
                        pool.indirect_dma_start(ring[q][2 + k], None, yslot_d,
                                                bass.IndirectOffsetOnAxis(ap=idx[j][:, 2 * q + k:2 * q + k + 1], axis=0))\
                            .then_inc(ld_g[q], 16)
                if live(c, 1):
                    o = (q - 1) % 4
                    wait(pool, s_cmv, c)
                    wait(pool, s_crstd, c - 1)
                    pool.tensor_scalar(cve, cmv[o][:, 1:2], EPS, None, ALU.add).then_inc(s_cve, 1)
                    wait(pool, s_cve, c)
                    pool.tensor_tensor(crstd[o], cve, neg, ALU.pow).then_inc(s_crstd, 1)

            def gather4(m, j):
                copy_index(groups + m + 1, m, j)
                for q in range(4):
                    gather(m * 4 + q, q, j)

            gather4(0, 0)
            gather4(1, 1)
            with loop(pool, 2, groups, 2) as m0:
                for j in range(2):
                    gather4(m0 + j, j)
            gather(TILES, 0, 0)


def kernel(**inputs):
    import numpy as np
    import concourse.bacc as bacc
    from concourse.bass_utils import run_bass_kernel_spmd

    a = {k: np.asarray(v) for k, v in inputs.items()}

    def chunks(m):
        return np.ascontiguousarray(m.reshape(-1, P, m.shape[1]).transpose(1, 0, 2))

    x = a["L0_attn_x"].reshape(N_TOK, D)
    w1 = np.concatenate([a["L0_ffn_spec_w1"], a["L0_ffn_shared_w1"][None]])
    w2 = np.concatenate([a["L0_ffn_spec_w2"], a["L0_ffn_shared_w2"][None]])
    b1 = np.concatenate([a["L0_ffn_spec_b1"], a["L0_ffn_shared_b1"][None]])
    b2 = np.concatenate([a["L0_ffn_spec_b2"], a["L0_ffn_shared_b2"][None]])
    ffn = np.concatenate([np.concatenate([chunks(u.T).reshape(P, -1), chunks(v.T).reshape(P, -1)], 1)
                          .reshape(P, EW // CHUNK, CHUNK).transpose(1, 0, 2) for u, v in zip(w1, w2)])
    p, n = np.arange(P), np.arange(EXPERTS * TILES)
    const = np.zeros((P, C_N), np.float32)
    const[:, C_ID:C_ID + P] = np.eye(P)
    const[:, C_MASK:C_MASK + P] = p[:, None] // HD == p[None] // HD
    const[:, C_MASK + P:C_MASK + CW] = p[:, None] // HD == np.arange(GH)[None]
    const[:, C_TRI:C_TRI + P] = p[:, None] < p[None]
    const[:, C_ONE:C_ONE + P] = 1
    const[:, C_REV:C_REV + EXPERTS] = EXPERTS - np.arange(EXPERTS)
    const[:, C_SEG:C_SEG + len(n)] = n % TILES != 0
    const[:, C_THR:C_THR + TILES // 2] = TILE * np.arange(TILES // 2)
    const[:, C_J:C_J + N_FFN] = np.arange(N_FFN) - HALF_SHARED
    const[:, C_NEG] = NEG
    const[:, C_RB:C_RB + EXPERTS] = a["L0_ffn_router_b"]
    arrays = {
        "xT": chunks(x.T), "x": x, "wqkvT": chunks(a["L0_attn_W_qkv"].T), "woutT": chunks(a["L0_attn_W_out"].T),
        "ffn": ffn, "b1": np.ascontiguousarray(b1.reshape(-1, FC, P).transpose(2, 0, 1).reshape(P, -1)),
        "b2": b2, "rwT": chunks(a["L0_ffn_router_w"].T), "const": const,
    }
    arrays = {k: np.ascontiguousarray(v) for k, v in arrays.items()}
    nc = bacc.Bacc("TRN2", target_bir_lowering=False, num_devices=1)
    args = [nc.dram_tensor(f"in_{k}", v.shape, F32, kind="ExternalInput").ap() for k, v in arrays.items()]
    out = nc.dram_tensor("out", (N_TOK, D), F32, kind="ExternalOutput").ap()
    build(nc, *args, out)
    r = run_bass_kernel_spmd(nc, [{f"in_{k}": v for k, v in arrays.items()}], core_ids=[0])
    return r.results[0]["out"].reshape(B, T, D)
```

```python
from contextlib import ExitStack, contextmanager

import concourse.bass as bass
from concourse import mybir

F32 = mybir.dt.float32
I32 = mybir.dt.int32
HALF = mybir.dt.bfloat16
ALU = mybir.AluOpType
ACT = mybir.ActivationFunctionType
X = mybir.AxisListType.X

P = 128
B, T, D = 4, 1024, 256
N_TOK = B * T
HEADS, HD = 16, 16
BUCKET = 64
FF = 1024
EXPERTS = 8
TOP = 2
KC = D // P
FC = FF // P
TILES = N_TOK // P
BT = T // P
GH = P // HD
CW = P + GH
NW = CW + GH
TILE = 2 * P
SLOT_TILES = TOP * N_TOK // TILE + EXPERTS - 1
SLOTS = SLOT_TILES * TILE
SHARED = N_TOK // TILE
HEAD = 10
TAIL = HEAD + SLOT_TILES
N_FFN = SHARED + SLOT_TILES
EW = 2 * KC * FF
CHUNK = 1024
W_CHUNKS = (EXPERTS + 1) * EW // CHUNK
NEG = -0.5
EPS = 1e-5
LN_LAG = 2
A_LAG = 4
SC = 2
GUARD = 1e-6 * HD ** 0.5

C_ID = 0
C_MASK = C_ID + P
C_TRI = C_MASK + CW
C_ONE = C_TRI + P
C_REV = C_ONE + P
C_SEG = C_REV + EXPERTS
C_THR = C_SEG + EXPERTS * TILES
C_J = C_THR + TILES // 2
C_NEG = C_J + SLOT_TILES
C_RB = C_NEG + 1
C_N = C_RB + EXPERTS


def build(nc, xT_d, x_d, wqkv_d, wout_d, ffn_d, b1_d, b2_d, rw_d, const_d, out_d):
    with ExitStack() as ctx:
        def sb(name, shape, dt):
            return ctx.enter_context(nc.sbuf_tensor(name, shape, dt))

        def sem(name):
            return ctx.enter_context(nc.semaphore(name))

        def sems(name, n):
            return [sem(f"{name}{i}") for i in range(n)]

        x2_d = nc.dram_tensor("x2_rows", (N_TOK, D), F32, kind="Internal").ap()
        tok_d = nc.dram_tensor("token_rows_split", (N_TOK, 2 * D), HALF, kind="Internal").ap()
        slot_d = nc.dram_tensor("slot_rows_split", (SLOTS, 2 * D), HALF, kind="Internal").ap()
        ytok_d = nc.dram_tensor("shared_out_rows", (N_TOK, D), F32, kind="Internal").ap()
        yslot_d = nc.dram_tensor("slot_out_rows", (SLOTS, D), F32, kind="Internal").ap()

        W = sb("weights", [P, (EXPERTS + 1) * 2 * EW], HALF)
        const = sb("const", [P, C_N], F32)
        ident_h = sb("ident_h", [P, P], HALF)
        b1 = sb("b1", [P, (EXPERTS + 1) * FC], F32)
        rw = sb("rw", [P, KC, EXPERTS], F32)
        zero = sb("zero", [P, SLOTS * 2 * D // (TILES * P)], HALF)
        logits = sb("logits", [P, TILES, EXPERTS], F32)
        gate = sb("gate", [P, TOP, TILES], F32)
        slot_f = sb("slot_f", [P, TILES, TOP], F32)
        slot_i = sb("slot_i", [P, TILES, TOP], I32)
        small = sb("small", [P, 16 * TILES], F32)
        expert_f = sb("expert_f", [P, SLOT_TILES], F32)
        expert_i = sb("expert_i", [P, SLOT_TILES], I32)
        ident = const[:, C_ID:C_ID + P]
        mask = const[:, C_MASK:C_MASK + CW]

        region = sb("region", [P, 12900], F32)
        at = {"A": 0, "B": 0}

        def carve(stage, cols, dt=F32):
            n = cols if dt is not HALF else cols // 2
            v = region[:, at[stage]:at[stage] + n]
            at[stage] += n
            assert at[stage] <= 12900, at
            return v if dt is F32 else v.bitcast(dt)

        xT = [carve("A", KC * TILE).rearrange("p (c n) -> p c n", c=KC) for _ in range(2)]
        xr = [carve("A", D) for _ in range(4)]
        stage = [carve("A", CHUNK) for _ in range(2)]
        wqkv = [carve("A", KC * 3 * D, HALF).rearrange("p (c n) -> p c n", c=KC) for _ in range(2)]
        wout = carve("A", KC * D).rearrange("p (c n) -> p c n", c=KC)
        xs = [carve("A", 2 * KC * P, HALF).rearrange("p (k n) -> p k n", k=2 * KC) for _ in range(2)]
        qs = carve("A", D)
        eq = [carve("A", D) for _ in range(2)]
        ek = [carve("A", D) for _ in range(2)]
        r_at = at["A"]
        vx = [carve("A", KC * CW).rearrange("p (g n) -> p g n", g=KC) for _ in range(2)]
        qT = [carve("A", D) for _ in range(2)]
        mc = [carve("A", KC * NW).rearrange("p (g n) -> p g n", g=KC) for _ in range(2)]
        attn_at = at["A"]
        attn = [carve("A", D) for _ in range(2)]
        attnT = [carve("A", D) for _ in range(2)]
        x2 = [carve("A", D) for _ in range(2)]
        x2s = [carve("A", 2 * D, HALF) for _ in range(2)]
        s = [carve("A", D) for _ in range(2)]
        x2T = carve("A", D)
        qmax = carve("A", HEADS)
        den = carve("A", HEADS)
        rden = carve("A", HEADS)
        stats = carve("A", 6)
        mv = [carve("A", 2) for _ in range(2)]
        ve = carve("A", 1)
        rstd = [carve("A", 1) for _ in range(2)]
        wqkv_f = region[:, attn_at:attn_at + KC * 3 * D].rearrange("p (c n) -> p c n", c=KC)
        n_te = TILES * EXPERTS
        r_tmp = [region[:, r_at + i * n_te:r_at + (i + 1) * n_te] for i in range(8)]

        rows = [carve("B", 2 * 2 * D, HALF).rearrange("p (h n) -> p h n", h=2) for _ in range(2)]
        XT = [carve("B", 4 * TILE, HALF).rearrange("p (k h n) -> p k h n", k=4, h=2) for _ in range(2)]
        hf = [carve("B", 2 * TILE) for _ in range(2)]
        hh = carve("B", FC * TILE, HALF).rearrange("p (f n) -> p f n", f=FC)
        hl = carve("B", FC * TILE, HALF).rearrange("p (f n) -> p f n", f=FC)
        yo = [carve("B", 2 * D).rearrange("p (h n) -> p h n", h=2) for _ in range(2)]
        b2 = [carve("B", D) for _ in range(2)]
        res = [carve("B", 2 * D).rearrange("p (h n) -> p h n", h=2) for _ in range(2)]
        sc_at = at["B"]
        g1 = [carve("B", D) for _ in range(4)]
        g2 = [carve("B", D) for _ in range(4)]
        acc = [carve("B", D) for _ in range(4)]
        normed = [carve("B", D) for _ in range(4)]
        b2s = carve("B", D)
        cstats = carve("B", 6)
        cmv = [carve("B", 2) for _ in range(4)]
        cve = carve("B", 1)
        crstd = [carve("B", 1) for _ in range(4)]
        idx = [carve("B", 8).bitcast(I32) for _ in range(4)]
        sc = [region[:, sc_at + i * SC * D:sc_at + (i + 1) * SC * D].bitcast(HALF)
              .rearrange("p (t n) -> p t n", t=SC) for i in range(4)]

        bank = [ctx.enter_context(nc.psum_tensor(f"bank{i}", [P, 512], F32)) for i in range(8)]
        Q, KV, EQT, CTX, NUM, ATT, WO, X2B = bank
        ctx_ps = CTX[:, 0:KC * CW].rearrange("p (g n) -> p g n", g=KC)
        num_ps = NUM[:, 0:KC * NW].rearrange("p (g n) -> p g n", g=KC)
        H = bank[0:4]
        Y = bank[4:6]
        TB = [b[:, :].bitcast(HALF)[:, 0:4 * P] for b in bank[6:8]]
        PRE, TOT = bank[4], bank[5]

        s_const, s_wq, s_w0, ld_b2s = sem("s_const"), sem("s_wq"), sem("s_w0"), sem("ld_b2s")
        s_init, s_passed = sem("s_init"), sem("s_passed")
        ld_xT, ld_xr, ld_w = sems("ld_xT", 2), sems("ld_xr", 4), sems("ld_w", 2)
        st_x2, st_rows, st_zero = sems("st_x2", 2), sems("st_rows", 2), sem("st_zero")
        s_q, s_kv, s_eqT, s_ctx = sem("s_q"), sem("s_kv"), sem("s_eqT"), sem("s_ctx")
        s_num, s_attnT, s_wo = sem("s_num"), sem("s_attnT"), sem("s_wo")
        s_x2T, s_lg = sem("s_x2T"), sem("s_lg")
        s_qmax, s_qsub, s_mask, s_den, s_attn = sem("s_qmax"), sem("s_qsub"), sem("s_mask"), sem("s_den"), sem("s_attn")
        s_res, s_st, s_mv, s_x2, s_lgo = sem("s_res"), sem("s_st"), sem("s_mv"), sem("s_x2"), sem("s_lgo")
        s_expk, s_vc, s_expq, s_qTe = sem("s_expk"), sem("s_vc"), sem("s_expq"), sem("s_qTe")
        s_aTe, s_x2Te, s_xh, s_x2h, s_wh = sem("s_aTe"), sem("s_x2Te"), sem("s_xh"), sem("s_x2h"), sem("s_wh")
        s_wl, s_ve, s_rstd, s_x2l, s_xl = sem("s_wl"), sem("s_ve"), sem("s_rstd"), sem("s_x2l"), sem("s_xl")
        s_r, s_rexp, s_rsub, s_hot, s_rank, s_ranked, s_slots = (
            sem("s_r"), sem("s_rexp"), sem("s_rsub"), sem("s_hot"), sem("s_rank"), sem("s_ranked"), sem("s_slots"))
        ld_rows, ld_b2, ld_res, st_y = sems("ld_rows", 2), sems("ld_b2", 2), sems("ld_res", 2), sems("st_y", 2)
        ld_sc, st_sc = sems("ld_sc", 4), sems("st_sc", 4)
        ld_acc, ld_g, st_out = sems("ld_acc", 4), sems("ld_g", 4), sems("st_out", 4)
        s_T, s_h, s_y = sem("s_T"), sem("s_h"), sem("s_y")
        s_XT, s_g, s_hh = sem("s_XT"), sem("s_g"), sem("s_hh")
        s_lo, s_ym, s_yo = sem("s_lo"), sem("s_ym"), sem("s_yo")
        s_idx, s_cadd, s_cst, s_cmv = sem("s_idx"), sem("s_cadd"), sem("s_cst"), sem("s_cmv")
        s_cfin, s_cve, s_crstd = sem("s_cfin"), sem("s_cve"), sem("s_crstd")

        block = ctx.enter_context(nc.Block())

        def wait(eng, semaphore, n, alone=False):
            if not isinstance(n, int) or n > 0:
                eng.wait_ge(semaphore, n)
            if not isinstance(n, int) and (alone or eng.engine == mybir.EngineType.Pool):
                eng.sem_inc(s_passed, 1)

        def live(t, lag, n=TILES):
            return not isinstance(t, int) or 0 <= t - lag < n

        @contextmanager
        def loop(eng, start, end, by):
            with eng.Fori(0, (end - start) // by) as n:
                yield n * by + start

        def steps_A(eng, step):
            for t in range(BT - 1):
                step(t, t)
            with loop(eng, BT - 1, TILES - 1, BT) as t0:
                for j in range(BT):
                    step(t0 + j, (BT - 1 + j) % BT)
            for t in range(TILES - 1, TILES + A_LAG):
                step(t, t % BT)

        def half_of(k):
            return (k // 2) % 2

        def loads(t, k, per, more):
            return (t - k) * (16 // per) + (k // per + more) * 16

        def one(view, i):
            return view[i] if isinstance(i, int) else view[bass.ds(i, 1)].rearrange("a p n -> p (a n)")

        tok_v = tok_d.rearrange("(t p) n -> t p n", p=P)
        x2_v = x2_d.rearrange("(t p) n -> t p n", p=P)
        x_v = x_d.rearrange("(t p) n -> t p n", p=P)
        out_v = out_d.rearrange("(t p) n -> t p n", p=P)
        yt_v = ytok_d.rearrange("(t p) n -> t p n", p=P)

        def ffn_tiles(eng, tile, first=lambda tile: tile(0, 0, None)):
            first(tile)
            with loop(eng, 2, HEAD, 2) as i0:
                for p in range(2):
                    tile(i0 + p, p, None)
            with loop(eng, HEAD, TAIL - 1, 2) as i0:
                for p in range(2):
                    tile(i0 + p, p, i0 + (p - HEAD))
            tile(TAIL - 1, (TAIL - 1) % 2, SLOT_TILES - 1)

        def tail_tiles(eng, tile):
            tile(TAIL, TAIL % 2, 0)
            with loop(eng, TAIL + 1, N_FFN - 1, 2) as i0:
                for j in range(2):
                    tile(i0 + j, (TAIL + 1 + j) % 2, i0 + (j - TAIL))
            tile(N_FFN - 1, (N_FFN - 1) % 2, N_FFN - 1 - TAIL)

        @block.sync
        def _(sp):
            sp.dma_start(wqkv_f, wqkv_d).then_inc(s_wq, 16)
            sp.dma_start(xT[0], xT_d[:, :, 0:TILE]).then_inc(ld_xT[0], 16)
            sp.dma_start(const[:], const_d).then_inc(s_const, 16)
            sp.dma_start(wout, wout_d).then_inc(s_w0, 16)
            sp.dma_start(rw[:], rw_d).then_inc(s_w0, 16)
            sp.dma_start(b1[:], b1_d).then_inc(s_w0, 16)
            sp.dma_start(stage[0], ffn_d[0]).then_inc(ld_w[0], 16)
            zero_v = slot_d.rearrange("s n -> (s n)").rearrange("(t p m) -> t p m", t=TILES, p=P)

            def step(t, k):
                if live(t, 0):
                    wait(sp, s_res, t - 3)
                    sp.dma_start(xr[k % 4], one(x_v, t)).then_inc(ld_xr[k % 4], 16)
                if k % 2 == 0 and live(t, -2) and (isinstance(t, int) or k < BT - 2):
                    wait(sp, s_xl, t)
                    src = xT_d[:, :, (t + 2) * P:(t + 4) * P] if isinstance(t, int) else \
                        xT_d[:, :, bass.ds((t + 2) * P, TILE)]
                    sp.dma_start(xT[half_of(k + 2)], src).then_inc(ld_xT[half_of(k + 2)], 16)
                if not isinstance(t, int) and k == BT - 2:
                    wait(sp, s_xl, t, alone=True)
                    sp.dma_start(xT[0], xT_d[:, :, bass.ds((t + 2) * P, TILE)]).then_inc(ld_xT[0], 16)
                if live(t, 4):
                    wait(sp, s_x2, t - 3)
                    sp.dma_start(one(x2_v, t - 4), x2[k % 2]).then_inc(st_x2[k % 2], 16)
                    wait(sp, s_x2l, t - 3)
                    sp.dma_start(one(tok_v, t - 4), x2s[k % 2]).then_inc(st_rows[k % 2], 16)
                if live(t, 0):
                    if k == 0 and isinstance(t, int):
                        sp.wait_ge(s_init, 1)
                    sp.dma_start(one(zero_v, t), zero[:]).then_inc(st_zero, 16)
                if live(t, -1, W_CHUNKS):
                    wait(sp, s_wl, t)
                    sp.dma_start(stage[(k + 1) % 2], one(ffn_d, t + 1)).then_inc(ld_w[(k + 1) % 2], 16)

            for t in range(BT):
                step(t, t)
            with loop(sp, BT, TILES - BT, BT) as t0:
                for k in range(BT):
                    step(t0 + k, k)
            for t in range(TILES - BT, TILES + A_LAG):
                step(t, t % BT)

            sp.wait_ge(s_lgo, TILES)
            for i in range(2):
                sp.wait_ge(st_x2[i], 16 * TILES // 2)
                sp.wait_ge(st_rows[i], 16 * TILES // 2)

            def tiles_of(view):
                return view.rearrange("(t h p) n -> t p h n", h=2, p=P)

            ffn_tok, ffn_slot, x2_t = tiles_of(tok_d), tiles_of(slot_d), tiles_of(x2_d)
            y_tok, y_slot = tiles_of(ytok_d), tiles_of(yslot_d)

            def of(view, i):
                return view[i] if isinstance(i, int) else view[bass.ds(i, 1)].rearrange("a p h n -> p (a h) n")

            def load_rows(i, p, view, j):
                wait(sp, s_T, 2 * (i - 1))
                sp.dma_start(rows[p], of(view, j)).then_inc(ld_rows[p], 16)

            def load_addend(i, p, n, j):
                if n is None:
                    sp.dma_start(res[j % 2 if isinstance(j, int) else p], of(x2_t, j))\
                        .then_inc(ld_res[j % 2 if isinstance(j, int) else p], 16)
                else:
                    e = sp.value_load(expert_i[0:1, n:n + 1] if isinstance(n, int) else expert_i[0:1, bass.ds(n, 1)],
                                      min_val=0, max_val=EXPERTS - 1)
                    sp.dma_start(b2[p], b2_d[bass.ds(e, 1), :].rearrange("a n -> (a n)").partition_broadcast(P))\
                        .then_inc(ld_b2[p], 16)

            def store_y(i, p, view, j):
                wait(sp, s_yo, 2 * (i + 1))
                sp.dma_start(of(view, j), yo[p]).then_inc(st_y[p], 16)

            sp.dma_start(b2s, b2_d[EXPERTS:EXPERTS + 1, :].rearrange("a n -> (a n)").partition_broadcast(P))\
                .then_inc(ld_b2s, 16)
            for i in range(2):
                load_rows(i, i, ffn_tok, i)
                load_addend(i, i, None, i)
            with loop(sp, 0, HEAD - 2, 2) as i0:
                for p in range(2):
                    i = i0 + p
                    load_rows(i + 2, p, ffn_tok, i + 2)
                    store_y(i, p, y_tok, i)
                    load_addend(i + 2, p, None, i + 2)
            for q in range(4):
                sp.wait_ge(st_sc[q], 16 * TOP * TILES // 4)
            for i in range(HEAD - 2, HEAD):
                p = i % 2
                load_rows(i + 2, p, ffn_slot, i + 2 - HEAD)
                store_y(i, p, y_tok, i)
                load_addend(i + 2, p, i + 2 - HEAD, None)
            with loop(sp, HEAD, TAIL - 3, 2) as i0:
                for p in range(2):
                    i = i0 + p
                    n = i0 + (p - HEAD)
                    load_rows(i + 2, p, ffn_slot, n + 2)
                    store_y(i, p, y_slot, n)
                    load_addend(i + 2, p, n + 2, None)
            for i in range(TAIL - 3, TAIL):
                p = i % 2
                if i + 2 < TAIL:
                    load_rows(i + 2, p, ffn_slot, i + 2 - HEAD)
                else:
                    load_rows(i + 2, p, ffn_tok, i + 2 - SLOT_TILES)
                store_y(i, p, y_slot, i - HEAD)
                load_addend(i + 2, p, i + 2 - HEAD if i + 2 < TAIL else None, i + 2 - SLOT_TILES)

            def combine_io(c, q):
                if live(c, 0):
                    wait(sp, s_cfin, c - 3)
                    sp.dma_start(acc[q], one(yt_v, c)).then_inc(ld_acc[q], 16)
                if live(c, 3):
                    o = (q - 3) % 4
                    wait(sp, s_cfin, c - 2)
                    sp.dma_start(one(out_v, c - 3), normed[o]).then_inc(st_out[o], 16)

            def tail(i, p, n):
                more = i + 2 < N_FFN
                j = i + (2 - SLOT_TILES)
                if more:
                    load_rows(i + 2, p, ffn_tok, j)
                wait(sp, st_y[1 - p], 8 * (i - p) + (16 if p else 0))
                for q in range(4):
                    combine_io(4 * n + q, q)
                store_y(i, p, y_tok, i - SLOT_TILES)
                if more:
                    a = (p - TAIL) % 2
                    sp.dma_start(res[a], of(x2_t, j)).then_inc(ld_res[a], 16)

            for i in range(TAIL, N_FFN):
                tail(i, i % 2, i - TAIL)
            done = 4 * (N_FFN - TAIL)
            sp.wait_ge(st_y[0], 16 * ((N_FFN + 1) // 2))
            sp.wait_ge(st_y[1], 16 * (N_FFN // 2))
            for c in range(done, TILES + 3):
                combine_io(c, c % 4)
            for q in range(4):
                sp.wait_ge(st_out[q], 16 * TILES // 4)
            sp.wait_ge(st_zero, 16 * TILES)

        @block.tensor
        def _(pe):
            terms = [(0, 0), (0, 1), (1, 0)]

            def context(u, k, r):
                n = 2 * u + r
                wait(pe, s_mask, n + 1)
                if r == 0:
                    wait(pe, s_expk, u + 1)
                    wait(pe, s_vc, u + 1)
                rows_ = slice(BUCKET * r, BUCKET * (r + 1))
                for g in range(KC):
                    mm = pe.matmul(ctx_ps[:, g, :], ek[k % 2][rows_, g * P:(g + 1) * P], vx[k % 2][rows_, g, :],
                                   start=(k == 0 and r == 0 and g == 0), stop=(k == BT - 1 and r == 1),
                                   skip_group_check=True)
                mm.then_inc(s_ctx, 1)

            def project(out, k, lo, hi):
                for n, (xp, wp) in enumerate(terms):
                    for c in range(KC):
                        mm = pe.matmul(out, xs[k % 2][:, xp * KC + c, :], wqkv[wp][:, c, lo:hi],
                                       start=(n == 0 and c == 0), stop=(n == len(terms) - 1 and c == KC - 1))
                return mm

            def step(t, k):
                if live(t, 1):
                    context(t - 1, (k - 1) % BT, 0)
                    wait(pe, s_expq, t)
                    wait(pe, s_qTe, t - 1)
                    for g in range(KC):
                        mm = pe.transpose(EQT[:, g * P:(g + 1) * P], eq[(k - 1) % 2][:, g * P:(g + 1) * P], ident)
                    mm.then_inc(s_eqT, 1)
                if live(t, 2):
                    wait(pe, s_attn, t - 1)
                    wait(pe, s_aTe, t - 2)
                    for g in range(KC):
                        mm = pe.transpose(ATT[:, g * P:(g + 1) * P], attn[k % 2][:, g * P:(g + 1) * P], ident)
                    mm.then_inc(s_attnT, 1)
                if live(t, 4):
                    wait(pe, s_x2, t - 3)
                    wait(pe, s_lgo, t - 4)
                    for g in range(KC):
                        mm = pe.transpose(X2B[:, g * P:(g + 1) * P], x2[k % 2][:, g * P:(g + 1) * P], ident)
                    mm.then_inc(s_x2T, 1)
                if live(t, 0):
                    wait(pe, s_xl, t + 1)
                    wait(pe, s_qsub, t)
                    project(Q[:, 0:D], k, 0, D).then_inc(s_q, 1)
                    wait(pe, s_vc, t)
                    project(KV[:, :], k, D, 3 * D).then_inc(s_kv, 1)
                if live(t, 1):
                    wait(pe, s_qTe, t)
                    wait(pe, s_attn, t - 1)
                    for r in range(2):
                        wait(pe, s_mask, 2 * (t - 1) + r + 1)
                        for g in range(KC):
                            o = g * P + BUCKET * r
                            mm = pe.matmul(num_ps[BUCKET * r:BUCKET * (r + 1), g, :],
                                           qT[(k - 1) % 2][:, o:o + BUCKET], mc[r][:, g, :], start=True, stop=True)
                    mm.then_inc(s_num, 1)
                    context(t - 1, (k - 1) % BT, 1)
                if live(t, 2):
                    wait(pe, s_aTe, t - 1)
                    wait(pe, s_res, t - 2)
                    for g in range(KC):
                        mm = pe.matmul(WO[:, 0:D], attnT[k % 2][:, g * P:(g + 1) * P], wout[:, g, :],
                                       start=(g == 0), stop=(g == KC - 1))
                    mm.then_inc(s_wo, 1)
                if live(t, 4):
                    wait(pe, s_x2Te, t - 3)
                    for g in range(KC):
                        mm = pe.matmul(X2B[:, D:D + EXPERTS], x2T[:, g * P:(g + 1) * P], rw[:, g, :],
                                       start=(g == 0), stop=(g == KC - 1))
                    mm.then_inc(s_lg, 1)

            pe.wait_ge(s_const, 16)
            pe.wait_ge(s_w0, 48)
            pe.wait_ge(s_init, 2)
            steps_A(pe, step)

            def turn(i, p):
                wait(pe, s_XT, 2 * i)
                wait(pe, ld_rows[p], 8 * (i - p) + 16)
                for h in range(2):
                    for k in range(4):
                        mm = pe.transpose(TB[h][:, k * P:(k + 1) * P], rows[p][:, h, k * P:(k + 1) * P], ident_h[:])
                    mm.then_inc(s_T, 1)

            def tile(i, p, n, more=True, ranks=False):
                if n is None:
                    base = EXPERTS * 2 * EW
                else:
                    e = pe.value_load(expert_i[0:1, n:n + 1] if isinstance(n, int) else expert_i[0:1, bass.ds(n, 1)],
                                      min_val=0, max_val=EXPERTS - 1)
                    base = pe.snap(e * (2 * EW))

                def weights(o, width):
                    return W[:, base + o:base + o + width] if n is None else W[:, bass.ds(base + o, width)]

                wait(pe, s_XT, 2 * i + 2)
                for f in range(FC):
                    wait(pe, s_g, 8 * i + f - 3)
                    for m, (part, xpart) in enumerate(terms):
                        for c in range(KC):
                            mm = pe.matmul(H[f % 4][:, 0:TILE], weights(part * EW + c * FF + f * P, P),
                                           XT[p][:, xpart * KC + c].rearrange("p h n -> p (h n)"),
                                           start=(m == 0 and c == 0), stop=(m == len(terms) - 1 and c == KC - 1))
                    mm.then_inc(s_h, 1)
                wait(pe, s_yo, 2 * i)
                if ranks:
                    pe.wait_ge(s_hot, 1)
                    pe.matmul(PRE[:, 0:n_te], const[:, C_TRI:C_TRI + P], r_tmp[0], start=True, stop=True)
                    pe.matmul(TOT[:, 0:n_te], const[:, C_ONE:C_ONE + P], r_tmp[0], start=True, stop=True)\
                        .then_inc(s_rank, 1)
                if more:
                    turn(i + 1, 1 - p)
                if ranks:
                    pe.wait_ge(s_ranked, 1)
                for f in range(FC):
                    if f % 2 == 0:
                        wait(pe, s_lo, 4 * i + f // 2 + 1)
                    for part, src in ((0, hh), (1, hh), (0, hl)):
                        w2 = weights(part * EW + KC * FF + f * D, D)
                        for h in range(2):
                            mm = pe.matmul(Y[h][:, 0:D], src[:, f, h * P:(h + 1) * P], w2,
                                           start=(f == 0 and part == 0 and src is hh),
                                           stop=(f == FC - 1 and src is hl))
                mm.then_inc(s_y, 1)

            def first(tile):
                turn(0, 0)
                pe.wait_ge(s_wl, W_CHUNKS)
                tile(0, 0, None)
                tile(1, 1, None, ranks=True)
                pe.wait_ge(s_slots, 1)

            ffn_tiles(pe, tile, first)
            tail_tiles(pe, lambda i, p, n: tile(i, p, None, not isinstance(i, int) or i + 1 < N_FFN))

        @block.scalar
        def _(act):
            def split_x(t, k):
                wait(act, ld_xT[half_of(k)], loads(t, k, 4, 1))
                wait(act, s_kv, t - 1)
                act.activation(xs[k % 2][:, 0:KC, :], xT[half_of(k)][:, :, (k % 2) * P:(k % 2 + 1) * P], ACT.Copy)\
                    .then_inc(s_xh, 1)

            def w_part(t, k, n):
                if isinstance(t, int):
                    o = t // 4 * (2 * EW) + t % 4 * CHUNK + n * EW
                    return W[:, o:o + CHUNK]
                return W[:, bass.ds((t - k) * (2 * EW // 4) + (k // 4 * (2 * EW) + k % 4 * CHUNK + n * EW), CHUNK)]

            def step(t, k):
                if live(t, 1):
                    wait(act, s_eqT, t)
                    wait(act, s_num, t - 2)
                    act.activation(qT[(k - 1) % 2], EQT[:, 0:D], ACT.Copy).then_inc(s_qTe, 1)
                if live(t, 2):
                    wait(act, s_attnT, t - 1)
                    wait(act, s_wo, t - 3)
                    act.activation(attnT[k % 2], ATT[:, 0:D], ACT.Copy).then_inc(s_aTe, 1)
                if live(t, 4):
                    wait(act, s_x2T, t - 3)
                    wait(act, s_lg, t - 4)
                    act.activation(x2T, X2B[:, 0:D], ACT.Copy).then_inc(s_x2Te, 1)
                if live(t, -1):
                    split_x(t + 1, (k + 1) % BT if isinstance(t, int) else k + 1)
                if live(t, 3):
                    wait(act, s_x2, t - 2)
                    wait(act, st_rows[(k + 1) % 2], loads(t, k, 2, -2 + k % 2))
                    act.activation(x2s[(k + 1) % 2][:, 0:D], x2[(k + 1) % 2], ACT.Copy).then_inc(s_x2h, 1)
                if live(t, 0):
                    wait(act, s_qsub, t + 1)
                    wait(act, s_eqT, t - 1)
                    act.activation(eq[k % 2], qs, ACT.Exp).then_inc(s_expq, 1)
                    wait(act, s_kv, t + 1)
                    wait(act, s_ctx, 2 * (t - 1))
                    act.activation(ek[k % 2], KV[:, 0:D], ACT.Exp).then_inc(s_expk, 1)
                    act.activation(vx[k % 2][:, :, 0:P], KV[:, D:2 * D].rearrange("p (g n) -> p g n", g=KC),
                                   ACT.Copy).then_inc(s_vc, 1)
                wait(act, ld_w[k % 2], loads(t, k, 2, 1))
                act.activation(w_part(t, k, 0), stage[k % 2], ACT.Copy).then_inc(s_wh, 1)

            act.wait_ge(s_init, 2)
            split_x(0, 0)
            steps_A(act, step)

            act.wait_ge(s_rsub, 1)
            act.activation(r_tmp[1], r_tmp[0], ACT.Exp).then_inc(s_rexp, 1)

            def evacuate(i, p):
                for h in range(2):
                    wait(act, s_T, 2 * i + h + 1)
                    act.activation(XT[p][:, :, h, :], TB[h].rearrange("p (k n) -> p k n", k=4), ACT.Copy)\
                        .then_inc(s_XT, 1)

            def high(i, g):
                wait(act, s_g, 8 * i + 2 * g + 2)
                if g == 0:
                    wait(act, s_y, i)
                act.activation(hh[:, 2 * g:2 * g + 2].rearrange("p f n -> p (f n)"), hf[g % 2], ACT.Copy)\
                    .then_inc(s_hh, 1)

            def tile(i, p, n, more=True):
                if n is not None:
                    e = act.value_load(expert_i[0:1, n:n + 1] if isinstance(n, int) else expert_i[0:1, bass.ds(n, 1)],
                                       min_val=0, max_val=EXPERTS - 1)
                for f in range(FC):
                    wait(act, s_h, 8 * i + f + 1)
                    if f % 2 == 0:
                        wait(act, s_lo, 4 * i + f // 2 - 1)
                    bias = b1[:, EXPERTS * FC + f:EXPERTS * FC + f + 1] if n is None else b1[:, bass.ds(e * FC + f, 1)]
                    act.activation(hf[f // 2 % 2][:, f % 2 * TILE:(f % 2 + 1) * TILE], H[f % 4][:, 0:TILE],
                                   ACT.Gelu_apprx_tanh, bias=bias).then_inc(s_g, 1)
                    if f % 2 == 0 and f:
                        high(i, f // 2 - 1)
                high(i, FC // 2 - 1)
                if more:
                    evacuate(i + 1, 1 - p)

            def first(tile):
                act.wait_ge(s_lgo, TILES)
                act.wait_ge(s_wl, W_CHUNKS)
                evacuate(0, 0)
                tile(0, 0, None)
                tile(1, 1, None)
                act.wait_ge(s_slots, 1)

            ffn_tiles(act, tile, first)
            tail_tiles(act, lambda i, p, n: tile(i, p, None, not isinstance(i, int) or i + 1 < N_FFN))

        @block.vector
        def _(dve):
            def context_before(k, r):
                if k == 0 and r == 0:
                    dve.memset(mc[0][:, :, 0:CW], 0.0).then_inc(s_mask, 1)
                else:
                    dve.tensor_tensor(mc[r][:, :, 0:CW], ctx_ps, mask.unsqueeze(1).to_broadcast([P, KC, CW]),
                                      ALU.mult).then_inc(s_mask, 1)

            def heads(ap):
                return ap.rearrange("p (h d) -> p h d", d=HD)

            def by_chunk(ap):
                return ap.rearrange("p (g h) -> p g h", g=KC)

            def step(t, k):
                if live(t, 1):
                    wait(dve, s_ctx, 2 * (t - 1) + 1)
                    wait(dve, s_num, t - 1)
                    context_before((k - 1) % BT, 1)
                if live(t, 3):
                    o = (k + 1) % 2
                    wait(dve, s_rstd, t - 2)
                    wait(dve, st_x2[o], loads(t, k, 2, -2 + k % 2))
                    wait(dve, s_x2l, t - 4)
                    wait(dve, s_x2T, t - 4)
                    dve.tensor_scalar(x2[o], s[o], mv[o][:, 0:1], rstd[o], ALU.subtract, ALU.mult).then_inc(s_x2, 1)
                if live(t, 0):
                    wait(dve, s_q, t + 1)
                    dve.tensor_reduce(qmax, heads(Q[:, 0:D]), X, ALU.max).then_inc(s_qmax, 1)
                    wait(dve, s_qmax, t + 1)
                    wait(dve, s_expq, t)
                    dve.tensor_tensor(heads(qs), heads(Q[:, 0:D]), qmax.unsqueeze(2).to_broadcast([P, HEADS, HD]),
                                      ALU.subtract).then_inc(s_qsub, 1)
                if live(t, 1):
                    wait(dve, s_num, t)
                    dve.tensor_copy(by_chunk(rden), num_ps[:, :, CW:NW]).then_inc(s_den, 1)
                    wait(dve, s_den, 3 * (t - 1) + 1)
                    dve.tensor_tensor(by_chunk(den), num_ps[:, :, P:CW], by_chunk(rden), ALU.max).then_inc(s_den, 1)
                    wait(dve, s_den, 3 * (t - 1) + 2)
                    dve.reciprocal(rden, den).then_inc(s_den, 1)
                    wait(dve, s_den, 3 * (t - 1) + 3)
                    wait(dve, s_attnT, t - 2)
                    dve.tensor_tensor(attn[(k - 1) % 2].rearrange("p (g h d) -> p g h d", g=KC, d=HD),
                                      num_ps[:, :, 0:P].rearrange("p g (h d) -> p g h d", d=HD),
                                      by_chunk(rden).unsqueeze(3).to_broadcast([P, KC, GH, HD]), ALU.mult)\
                        .then_inc(s_attn, 1)
                if live(t, 0):
                    wait(dve, s_ctx, 2 * t)
                    wait(dve, s_num, t)
                    context_before(k, 0)
                if live(t, 2):
                    wait(dve, s_wo, t - 1)
                    wait(dve, ld_xr[(k - 2) % 4], loads(t, k, 4, 1 if k % 4 >= 2 else 0))
                    dve.tensor_tensor(s[k % 2], WO[:, 0:D], xr[(k - 2) % 4], ALU.add).then_inc(s_res, 1)
                    wait(dve, s_res, t - 1)
                    dve.bn_stats(stats, s[k % 2]).then_inc(s_st, 1)
                    wait(dve, s_rstd, t - 3)
                    wait(dve, s_st, t - 1, alone=True)
                    dve.bn_aggr(mv[k % 2], stats).then_inc(s_mv, 1)
                if live(t, 4):
                    wait(dve, s_lg, t - 3)
                    row = logits[:, t - 4, :] if isinstance(t, int) else \
                        logits[:, bass.ds(t - 4, 1), :].rearrange("p a e -> p (a e)")
                    dve.tensor_tensor(row, X2B[:, D:D + EXPERTS], const[:, C_RB:C_RB + EXPERTS], ALU.add)\
                        .then_inc(s_lgo, 1)

            dve.memset(zero[:], 0.0).then_inc(s_init, 1)
            for j in range(2):
                dve.memset(vx[j][:, :, P:CW], 1.0)
            dve.wait_ge(s_wq, 16)
            dve.tensor_copy(wqkv[0], wqkv_f).then_inc(s_r, 1)
            dve.wait_ge(s_const, 16)
            for j in range(2):
                for g in range(KC):
                    dve.tensor_scalar(mc[j][:, g, CW:NW], mask[:, P:CW], GUARD, None, ALU.mult)
            dve.tensor_copy(ident_h[:], ident)
            dve.wait_ge(s_r, 1)
            dve.tensor_tensor(wqkv[1], wqkv_f, wqkv[0], ALU.subtract).then_inc(s_init, 1)
            steps_A(dve, step)

            done = [1]

            def then(ins):
                done[0] += 1
                ins.then_inc(s_r, 1)
                dve.wait_ge(s_r, done[0])

            def te(ap):
                return ap.rearrange("p (t e) -> p t e", e=EXPERTS)

            def et(ap):
                return ap.rearrange("p (e t) -> p e t", t=TILES)

            def over_e(ap):
                return ap.unsqueeze(2).to_broadcast([P, TILES, EXPERTS])

            col = [small[:, i * TILES:(i + 1) * TILES] for i in range(8)]
            top1, top2, first_, inv, summed = col[0:5]
            rev = const[:, C_REV:C_REV + EXPERTS].unsqueeze(1).to_broadcast([P, TILES, EXPERTS])
            prob, hot1, hot2, tmp = r_tmp[1], r_tmp[2], r_tmp[3], r_tmp[4]

            def router_softmax():
                dve.wait_ge(s_rexp, 1)
                then(dve.tensor_reduce(summed, te(prob), X, ALU.add))
                then(dve.reciprocal(inv, summed))
                then(dve.tensor_tensor(te(prob), te(prob), over_e(inv), ALU.mult))

            def pick(top, hot):
                then(dve.tensor_reduce(top, te(prob), X, ALU.max))
                then(dve.tensor_tensor(te(tmp), te(prob), over_e(top), ALU.is_equal))
                then(dve.tensor_tensor(te(tmp), te(tmp), rev, ALU.mult))
                then(dve.tensor_reduce(first_, te(tmp), X, ALU.max))
                then(dve.tensor_tensor(te(hot), rev, over_e(first_), ALU.is_equal))

            def pick_first():
                pick(top1, hot1)
                then(dve.scalar_tensor_tensor(prob, hot1, -2.0, prob, ALU.mult, ALU.add))

            def pick_second():
                pick(top2, hot2)
                dve.tensor_tensor(r_tmp[0], hot1, hot2, ALU.add).then_inc(s_hot, 1)

            def gates():
                then(dve.tensor_tensor(summed, top1, top2, ALU.add))
                then(dve.reciprocal(inv, summed))
                then(dve.tensor_tensor(gate[:, 0, :], top1, inv, ALU.mult))
                then(dve.tensor_tensor(gate[:, 1, :], top2, inv, ALU.mult))

            def place():
                tot, upto, excl = r_tmp[5], r_tmp[6], r_tmp[7]
                n_e, end_e, base_e = col[5][:, 0:EXPERTS], col[6][:, 0:EXPERTS], col[7][:, 0:EXPERTS]
                dve.wait_ge(s_rank, 1)
                then(dve.tensor_copy(et(tot), TOT[:, 0:n_te].rearrange("p (t e) -> p e t", e=EXPERTS)))
                dve.tensor_copy(tmp, PRE[:, 0:n_te]).then_inc(s_ranked, 1)
                then(dve.tensor_tensor_scan(upto, const[:, C_SEG:C_SEG + n_te], tot, 0.0, ALU.mult, ALU.add))
                then(dve.tensor_tensor(excl, upto, tot, ALU.subtract))
                nthr = TILES // 2
                over = tot[:, 0:EXPERTS * nthr].rearrange("p (e j) -> p e j", j=nthr)
                then(dve.tensor_tensor(over, et(upto)[:, :, TILES - 1].unsqueeze(2).to_broadcast([P, EXPERTS, nthr]),
                                       const[:, C_THR:C_THR + nthr].unsqueeze(1).to_broadcast([P, EXPERTS, nthr]),
                                       ALU.is_gt))
                then(dve.tensor_reduce(n_e, over, X, ALU.add))
                then(dve.tensor_tensor_scan(end_e, const[:, C_ONE:C_ONE + EXPERTS], n_e, 0.0, ALU.mult, ALU.add))
                then(dve.tensor_tensor(base_e, end_e, n_e, ALU.subtract))
                then(dve.tensor_scalar(base_e, base_e, float(TILE), None, ALU.mult))
                then(dve.tensor_tensor(et(excl), et(excl), base_e.unsqueeze(2).to_broadcast([P, EXPERTS, TILES]),
                                       ALU.add))
                dve.wait_ge(s_ranked, 1)
                then(dve.tensor_tensor(te(tmp), te(tmp), excl.rearrange("p (e t) -> p t e", t=TILES), ALU.add))
                for j, hot in enumerate((hot1, hot2)):
                    then(dve.tensor_tensor(hot, hot, tmp, ALU.mult))
                    then(dve.tensor_reduce(slot_f[:, :, j], te(hot), X, ALU.add))
                then(dve.tensor_copy(slot_i[:].rearrange("p t j -> p (t j)"), slot_f[:].rearrange("p t j -> p (t j)")))
                for lo in range(0, SLOT_TILES, TILES):
                    n = min(TILES, SLOT_TILES - lo)
                    a = te(r_tmp[5])[:, 0:n, :]
                    then(dve.tensor_tensor(a, end_e.unsqueeze(1).to_broadcast([P, n, EXPERTS]),
                                           const[:, C_J + lo:C_J + lo + n].unsqueeze(2)
                                           .to_broadcast([P, n, EXPERTS]), ALU.is_le))
                    then(dve.tensor_reduce(expert_f[:, lo:lo + n], a, X, ALU.add))
                then(dve.tensor_scalar(expert_f[:], expert_f[:], float(EXPERTS - 1), None, ALU.min))
                dve.tensor_copy(expert_i[:], expert_f[:]).then_inc(s_slots, 1)

            def low(i, g):
                wait(dve, s_hh, 4 * i + g + 1)
                dve.tensor_tensor(hl[:, 2 * g:2 * g + 2].rearrange("p f n -> p (f n)"), hf[g % 2],
                                  hh[:, 2 * g:2 * g + 2].rearrange("p f n -> p (f n)"), ALU.subtract)\
                    .then_inc(s_lo, 1)

            def outputs(i, p, n, a):
                wait(dve, s_y, i + 1)
                wait(dve, st_y[p], 8 * (i - p))
                if n is None:
                    for h in range(2):
                        dve.tensor_tensor(yo[p][:, h, :], Y[h][:, 0:D], b2s, ALU.add).then_inc(s_ym, 1)
                    m = i if isinstance(i, int) and i < HEAD else None
                    shared = m if m is not None else i if a[1] == 0 else i - SLOT_TILES
                    wait(dve, ld_res[a[0]], a[2])
                    wait(dve, s_ym, 2 * shared + 2)
                    for h in range(2):
                        dve.tensor_tensor(yo[p][:, h, :], yo[p][:, h, :], res[a[0]][:, h, :], ALU.add).then_inc(s_yo, 1)
                else:
                    wait(dve, ld_b2[p], 8 * (n - p) + 16)
                    for h in range(2):
                        dve.tensor_tensor(yo[p][:, h, :], Y[h][:, 0:D], b2[p], ALU.add).then_inc(s_yo, 1)

            def gate_of(j, c):
                return gate[:, j, c:c + 1] if isinstance(c, int) else gate[:, j, bass.ds(c, 1)]

            def combine(c, q):
                if live(c, 0):
                    wait(dve, ld_acc[q], 4 * (c - q) + 16)
                    wait(dve, ld_g[q], 8 * (c - q) + 32)
                    dve.scalar_tensor_tensor(acc[q], g1[q], gate_of(0, c), acc[q], ALU.mult, ALU.add)\
                        .then_inc(s_cadd, 1)
                    wait(dve, s_cadd, 2 * c + 1)
                    dve.scalar_tensor_tensor(acc[q], g2[q], gate_of(1, c), acc[q], ALU.mult, ALU.add)\
                        .then_inc(s_cadd, 1)
                if live(c, LN_LAG):
                    o = (q - LN_LAG) % 4
                    wait(dve, s_crstd, c - LN_LAG + 1)
                    wait(dve, st_out[o], 4 * (c - LN_LAG - o))
                    dve.tensor_scalar(normed[o], acc[o], cmv[o][:, 0:1], crstd[o], ALU.subtract, ALU.mult)\
                        .then_inc(s_cfin, 1)
                if live(c, 0):
                    wait(dve, s_cadd, 2 * c + 2)
                    dve.bn_stats(cstats, acc[q]).then_inc(s_cst, 1)
                    wait(dve, s_cst, c + 1, alone=True)
                    dve.bn_aggr(cmv[q], cstats).then_inc(s_cmv, 1)

            def tile(i, p, n, c0=None, between=()):
                for g in range(4):
                    low(i, g)
                    if c0 is not None:
                        combine(c0 + g, g)
                    if g < len(between):
                        between[g]()
                if c0 is None:
                    outputs(i, p, n, (p, 0, 8 * (i - p) + 16))
                else:
                    a = (p - TAIL) % 2
                    outputs(i, p, None, (a, 1, 8 * (i - TAIL - a) + 16 * (HEAD // 2 + 1)))

            def first(tile):
                dve.wait_ge(s_lgo, TILES)
                then(dve.tensor_reduce(top1, logits[:], X, ALU.max))
                dve.tensor_tensor(te(r_tmp[0]), logits[:], over_e(top1), ALU.subtract).then_inc(s_rsub, 1)
                router_softmax()
                dve.wait_ge(ld_b2s, 16)
                tile(0, 0, None, between=(pick_first, pick_second))
                tile(1, 1, None, between=(gates, lambda: None, lambda: None, place))

            ffn_tiles(dve, tile, first)
            for i in range(TAIL, N_FFN):
                tile(i, i % 2, None, 4 * (i - TAIL))
            for c in range(4 * (N_FFN - TAIL), TILES + LN_LAG):
                combine(c, c % 4)

        @block.gpsimd
        def _(pool):
            neg = const[:, C_NEG:C_NEG + 1]

            def split_x(t, k):
                wait(pool, s_xh, t + 1)
                pool.tensor_tensor(xs[k % 2][:, KC:2 * KC, :], xT[half_of(k)][:, :, (k % 2) * P:(k % 2 + 1) * P],
                                   xs[k % 2][:, 0:KC, :], ALU.subtract).then_inc(s_xl, 1)

            def w_part(t, k, n):
                if isinstance(t, int):
                    o = t // 4 * (2 * EW) + t % 4 * CHUNK + n * EW
                    return W[:, o:o + CHUNK]
                kk = k % BT
                return W[:, bass.ds((t - k) * (2 * EW // 4) + ((kk // 4 - (2 if k < 0 else 0)) * (2 * EW)
                                                               + kk % 4 * CHUNK + n * EW), CHUNK)]

            def low_weights(t, k):
                wait(pool, s_wh, t + 1)
                pool.tensor_tensor(w_part(t, k, 1), stage[k % 2], w_part(t, k, 0), ALU.subtract).then_inc(s_wl, 1)

            def step(t, k):
                if live(t, -1):
                    split_x(t + 1, (k + 1) % BT if isinstance(t, int) else k + 1)
                if live(t, 3):
                    o = (k + 1) % 2
                    wait(pool, s_x2h, t - 2)
                    pool.tensor_tensor(x2s[o][:, D:2 * D], x2[o], x2s[o][:, 0:D], ALU.subtract).then_inc(s_x2l, 1)
                if live(t, 1, W_CHUNKS):
                    low_weights(t - 1, k - 1)
                if live(t, 2):
                    wait(pool, s_mv, t - 1)
                    wait(pool, s_rstd, t - 2)
                    pool.tensor_scalar(ve, mv[k % 2][:, 1:2], EPS, None, ALU.add).then_inc(s_ve, 1)
                    wait(pool, s_ve, t - 1)
                    wait(pool, s_x2, t - 3)
                    pool.tensor_tensor(rstd[k % 2], ve, neg, ALU.pow).then_inc(s_rstd, 1)

            pool.wait_ge(s_const, 16)
            split_x(0, 0)
            steps_A(pool, step)
            low_weights(W_CHUNKS - 1, (W_CHUNKS - 1) % BT)

            sc_v = tok_d.rearrange("(g t p) n -> g p t n", t=SC, p=P)

            def copy_index(n, g, j, tiles):
                src = slot_i[:, tiles * g:tiles * (g + 1), :] if isinstance(g, int) else \
                    slot_i[:, bass.ds(g * tiles, tiles), :]
                pool.tensor_copy(idx[j][:, 0:TOP * tiles], src.rearrange("p t j -> p (t j)")).then_inc(s_idx, 1)
                wait(pool, s_idx, n)

            def load_sc(g, j):
                src = sc_v[g] if isinstance(g, int) else sc_v[bass.ds(g, 1)].rearrange("a p t n -> p (a t) n")
                wait(pool, st_sc[j], 16 * TOP * SC // 4 * (g - j))
                pool.dma_start(sc[j], src).then_inc(ld_sc[j], 16)

            def scatter(g, j):
                copy_index(g + 1, g, j, SC)
                wait(pool, ld_sc[j], 4 * (g - j) + 16)
                for t in range(SC):
                    for k in range(TOP):
                        pool.indirect_dma_start(slot_d, bass.IndirectOffsetOnAxis(ap=idx[j][:, 2 * t + k:2 * t + k + 1], axis=0),
                                                sc[j][:, t, :], None).then_inc(st_sc[j], 16)

            pool.wait_ge(s_slots, 1)
            pool.wait_ge(st_zero, 16 * TILES)
            for i in range(2):
                pool.wait_ge(st_rows[i], 16 * TILES // 2)
                pool.wait_ge(st_x2[i], 16 * TILES // 2)
            groups = TILES // SC
            for j in range(4):
                load_sc(j, j)
            with loop(pool, 0, groups - 4, 4) as g0:
                for j in range(4):
                    scatter(g0 + j, j)
                    if j:
                        load_sc(g0 + (j + 3), j - 1)
                load_sc(g0 + 7, 3)
            for g in range(groups - 4, groups):
                scatter(g, g % 4)

            for p in range(2):
                pool.wait_ge(st_y[p], 16 * ((TAIL + 1 - p) // 2))
            for q in range(4):
                pool.wait_ge(st_sc[q], 16 * TOP * TILES // 4)

            def gather(c, q, j):
                if live(c, 0):
                    wait(pool, s_cadd, 2 * (c - 3))
                    for k, g in enumerate((g1, g2)):
                        pool.indirect_dma_start(g[q], None, yslot_d,
                                                bass.IndirectOffsetOnAxis(ap=idx[j][:, 2 * q + k:2 * q + k + 1], axis=0))\
                            .then_inc(ld_g[q], 16)
                if live(c, LN_LAG):
                    o = (q - LN_LAG) % 4
                    wait(pool, s_cmv, c - LN_LAG + 1)
                    wait(pool, s_crstd, c - LN_LAG)
                    pool.tensor_scalar(cve, cmv[o][:, 1:2], EPS, None, ALU.add).then_inc(s_cve, 1)
                    wait(pool, s_cve, c - LN_LAG + 1)
                    pool.tensor_tensor(crstd[o], cve, neg, ALU.pow).then_inc(s_crstd, 1)

            def gather4(m, j):
                copy_index(m + (groups + 1), m, j, 4)
                for q in range(4):
                    gather(m * 4 + q, q, j)

            gather4(0, 0)
            gather4(1, 1)
            with loop(pool, 2, TILES // 4, 2) as m0:
                for j in range(2):
                    gather4(m0 + j, j)
            for c in range(TILES, TILES + LN_LAG):
                gather(c, c % 4, 0)


def kernel(**inputs):
    import numpy as np
    import concourse.bacc as bacc
    from concourse.bass_utils import run_bass_kernel_spmd

    a = {k: np.asarray(v) for k, v in inputs.items()}

    def chunks(m):
        return np.ascontiguousarray(m.reshape(-1, P, m.shape[1]).transpose(1, 0, 2))

    x = a["L0_attn_x"].reshape(N_TOK, D)
    w1 = np.concatenate([a["L0_ffn_spec_w1"], a["L0_ffn_shared_w1"][None]])
    w2 = np.concatenate([a["L0_ffn_spec_w2"], a["L0_ffn_shared_w2"][None]])
    b1 = np.concatenate([a["L0_ffn_spec_b1"], a["L0_ffn_shared_b1"][None]])
    b2 = np.concatenate([a["L0_ffn_spec_b2"], a["L0_ffn_shared_b2"][None]])
    ffn = np.concatenate([np.concatenate([chunks(u.T).reshape(P, -1), chunks(v.T).reshape(P, -1)], 1)
                          .reshape(P, EW // CHUNK, CHUNK).transpose(1, 0, 2) for u, v in zip(w1, w2)])
    p, n = np.arange(P), np.arange(EXPERTS * TILES)
    const = np.zeros((P, C_N), np.float32)
    const[:, C_ID:C_ID + P] = np.eye(P)
    const[:, C_MASK:C_MASK + P] = p[:, None] // HD == p[None] // HD
    const[:, C_MASK + P:C_MASK + CW] = p[:, None] // HD == np.arange(GH)[None]
    const[:, C_TRI:C_TRI + P] = p[:, None] < p[None]
    const[:, C_ONE:C_ONE + P] = 1
    const[:, C_REV:C_REV + EXPERTS] = EXPERTS - np.arange(EXPERTS)
    const[:, C_SEG:C_SEG + len(n)] = n % TILES != 0
    const[:, C_THR:C_THR + TILES // 2] = TILE * np.arange(TILES // 2)
    const[:, C_J:C_J + SLOT_TILES] = np.arange(SLOT_TILES)
    const[:, C_NEG] = NEG
    const[:, C_RB:C_RB + EXPERTS] = a["L0_ffn_router_b"]
    arrays = {
        "xT": chunks(x.T), "x": x, "wqkvT": chunks(a["L0_attn_W_qkv"].T), "woutT": chunks(a["L0_attn_W_out"].T),
        "ffn": ffn, "b1": np.ascontiguousarray(b1.reshape(-1, FC, P).transpose(2, 0, 1).reshape(P, -1)),
        "b2": b2, "rwT": chunks(a["L0_ffn_router_w"].T), "const": const,
    }
    arrays = {k: np.ascontiguousarray(v) for k, v in arrays.items()}
    nc = bacc.Bacc("TRN2", target_bir_lowering=False, num_devices=1)
    args = [nc.dram_tensor(f"in_{k}", v.shape, F32, kind="ExternalInput").ap() for k, v in arrays.items()]
    out = nc.dram_tensor("out", (N_TOK, D), F32, kind="ExternalOutput").ap()
    build(nc, *args, out)
    r = run_bass_kernel_spmd(nc, [{f"in_{k}": v for k, v in arrays.items()}], core_ids=[0])
    return r.results[0]["out"].reshape(B, T, D)
```

```python
from contextlib import ExitStack, contextmanager

import concourse.bass as bass
from concourse import mybir

F32 = mybir.dt.float32
I32 = mybir.dt.int32
HALF = mybir.dt.bfloat16
ALU = mybir.AluOpType
ACT = mybir.ActivationFunctionType
X = mybir.AxisListType.X

P = 128
B, T, D = 4, 1024, 256
N_TOK = B * T
HEADS, HD = 16, 16
BUCKET = 64
FF = 1024
EXPERTS = 8
TOP = 2
KC = D // P
FC = FF // P
TILES = N_TOK // P
BT = T // P
GH = P // HD
CW = P + GH
NW = CW + GH
TILE = 2 * P
SLOT_TILES = TOP * N_TOK // TILE + EXPERTS - 1
SLOTS = SLOT_TILES * TILE
SHARED = N_TOK // TILE
HEAD = 8
TAIL = HEAD + SLOT_TILES
N_FFN = SHARED + SLOT_TILES
EW = 2 * KC * FF
ALL_W = (EXPERTS + 1) * EW
W_CHUNKS = TILES
CHUNK = ALL_W // W_CHUNKS
REGION = 13424
NEG = -0.5
EPS = 1e-5
A_LAG = 5
GROUP = 4
GROUPS = TILES // GROUP
IN_YO = TILES - GROUP
OFFSET = 1
GUARD = 1e-6 * HD ** 0.5

C_ID = 0
C_MASK = C_ID + P
C_TRI = C_MASK + CW
C_ONE = C_TRI + P
C_REV = C_ONE + P
C_SEG = C_REV + EXPERTS
C_THR = C_SEG + EXPERTS * TILES
C_J = C_THR + TILES // 2
C_NEG = C_J + SLOT_TILES
C_RB = C_NEG + 1
C_N = C_RB + EXPERTS


def build(nc, xT_d, x_d, wqkv_d, wout_d, ffn_d, b1_d, b2_d, rw_d, const_d, out_d):
    with ExitStack() as ctx:
        def sb(name, shape, dt):
            return ctx.enter_context(nc.sbuf_tensor(name, shape, dt))

        def sem(name):
            return ctx.enter_context(nc.semaphore(name))

        def sems(name, n):
            return [sem(f"{name}{i}") for i in range(n)]

        res_d = nc.dram_tensor("residual_rows", (N_TOK, D), F32, kind="Internal").ap()
        tok_d = nc.dram_tensor("token_rows_split", (N_TOK, 2 * D), HALF, kind="Internal").ap()
        slot_d = nc.dram_tensor("slot_rows_split", (SLOTS, 2 * D), HALF, kind="Internal").ap()
        ytok_d = nc.dram_tensor("shared_out_rows", (N_TOK, D), F32, kind="Internal").ap()
        yslot_d = nc.dram_tensor("slot_out_rows", (SLOTS, D), F32, kind="Internal").ap()

        W = sb("weights", [P, 2 * ALL_W], HALF)
        const = sb("const", [P, C_N], F32)
        ident_h = sb("ident_h", [P, P], HALF)
        b1 = sb("b1", [P, (EXPERTS + 1) * FC], F32)
        b2s = sb("b2_shared", [P, D], F32)
        rw = sb("rw", [P, KC, EXPERTS], F32)
        zero = sb("zero", [P, SLOTS * 2 * D // (TILES * P)], HALF)
        logits = sb("logits", [P, TILES, EXPERTS], F32)
        gate = sb("gate", [P, TOP, TILES], F32)
        slot_f = sb("slot_f", [P, TILES, TOP], F32)
        slot_i = sb("slot_i", [P, TILES, TOP], I32)
        small = sb("small", [P, 16 * TILES], F32)
        expert_f = sb("expert_f", [P, SLOT_TILES], F32)
        expert_i = sb("expert_i", [P, SLOT_TILES], I32)
        ident = const[:, C_ID:C_ID + P]
        mask = const[:, C_MASK:C_MASK + CW]

        region = sb("region", [P, REGION], F32)
        at = {"A": 0, "B": 0}

        def carve(stage, cols, dt=F32):
            n = cols if dt is not HALF else cols // 2
            v = region[:, at[stage]:at[stage] + n]
            at[stage] += n
            assert at[stage] <= REGION, at
            return v if dt is F32 else v.bitcast(dt)

        xT = [carve("A", KC * TILE).rearrange("p (c n) -> p c n", c=KC) for _ in range(2)]
        xr = [carve("A", D) for _ in range(4)]
        stage = [carve("A", CHUNK) for _ in range(2)]
        wqkv = [carve("A", KC * 3 * D, HALF).rearrange("p (c n) -> p c n", c=KC) for _ in range(2)]
        wout = carve("A", KC * D).rearrange("p (c n) -> p c n", c=KC)
        xs = [carve("A", 2 * KC * P, HALF).rearrange("p (k n) -> p k n", k=2 * KC) for _ in range(2)]
        qs = carve("A", D)
        eq = [carve("A", D) for _ in range(2)]
        ek = [carve("A", D) for _ in range(2)]
        x2 = [carve("A", D) for _ in range(2)]
        x2s = [carve("A", 2 * D, HALF) for _ in range(2)]
        x2b = [carve("A", D) for _ in range(2)]
        r_at = at["A"]
        vx = [carve("A", KC * CW).rearrange("p (g n) -> p g n", g=KC) for _ in range(2)]
        qT = [carve("A", D) for _ in range(2)]
        mc = [carve("A", KC * NW).rearrange("p (g n) -> p g n", g=KC) for _ in range(2)]
        attn_at = at["A"]
        attn = [carve("A", D) for _ in range(2)]
        attnT = [carve("A", D) for _ in range(2)]
        s = [carve("A", D) for _ in range(2)]
        x2T = carve("A", D)
        qmax = carve("A", HEADS)
        den = carve("A", HEADS)
        rden = carve("A", HEADS)
        stats = carve("A", 6)
        mv = [carve("A", 2) for _ in range(2)]
        ve = [carve("A", 1) for _ in range(2)]
        rstd = [carve("A", 1) for _ in range(2)]
        wqkv_f = region[:, attn_at:attn_at + KC * 3 * D].rearrange("p (c n) -> p c n", c=KC)
        n_te = TILES * EXPERTS
        r_tmp = [region[:, r_at + i * n_te:r_at + (i + 1) * n_te] for i in range(8)]

        rows = [carve("B", 2 * 2 * D, HALF).rearrange("p (h n) -> p h n", h=2) for _ in range(2)]
        XT = [carve("B", 4 * TILE, HALF).rearrange("p (k h n) -> p k h n", k=4, h=2) for _ in range(2)]
        hf = [carve("B", 2 * TILE) for _ in range(2)]
        hh = carve("B", FC * TILE, HALF).rearrange("p (f n) -> p f n", f=FC)
        hl = carve("B", FC * TILE, HALF).rearrange("p (f n) -> p f n", f=FC)
        yo = [carve("B", 2 * D).rearrange("p (h n) -> p h n", h=2) for _ in range(2)]
        b2 = [carve("B", D) for _ in range(2)]
        res = [carve("B", 2 * D).rearrange("p (h n) -> p h n", h=2) for _ in range(2)]
        sc_at = at["B"]
        spare = zero[:, 0:2 * TOP * D].bitcast(F32)
        g1 = [carve("B", D) for _ in range(2 * GROUP - 1)] + [spare[:, 0:D]]
        g2 = [carve("B", D) for _ in range(2 * GROUP - 1)] + [spare[:, D:2 * D]]
        acc = [carve("B", D) for _ in range(2 * GROUP)]
        cstats = carve("B", 6)
        cmv = carve("B", 2 * GROUP * 2).rearrange("p (q n) -> p q n", n=2)
        cve = [carve("B", GROUP) for _ in range(2)]
        crstd = [carve("B", GROUP) for _ in range(2)]
        idx = [carve("B", TOP * GROUP).bitcast(I32) for _ in range(4)]
        sc = [region[:, sc_at + i * GROUP * D:sc_at + (i + 1) * GROUP * D].bitcast(HALF)
              .rearrange("p (t n) -> p t n", t=GROUP) for i in range(4)]
        assert r_at >= sc_at + 2 * GROUP * D and at["A"] >= r_at + 8 * n_te

        bank = [ctx.enter_context(nc.psum_tensor(f"bank{i}", [P, 512], F32)) for i in range(8)]
        Q, KV, EQT, CTX, NUM, ATT, WO, X2B = bank
        ctx_ps = CTX[:, 0:KC * CW].rearrange("p (g n) -> p g n", g=KC)
        num_ps = NUM[:, 0:KC * NW].rearrange("p (g n) -> p g n", g=KC)
        H = bank[0:4]
        Y = bank[4:6]
        TB = [b[:, :].bitcast(HALF)[:, 0:4 * P] for b in bank[6:8]]
        PRE, TOT = bank[4], bank[5]

        s_const, s_wq, s_w0, ld_b2s = sem("s_const"), sem("s_wq"), sem("s_w0"), sem("ld_b2s")
        s_init, s_wqh, s_passed = sem("s_init"), sem("s_wqh"), sem("s_passed")
        ld_xT, ld_xr, ld_w = sems("ld_xT", 2), sems("ld_xr", 4), sems("ld_w", 2)
        st_res, st_rows, st_zero = sems("st_res", 2), sems("st_rows", 2), sem("st_zero")
        s_q, s_kv, s_eqT, s_ctx = sem("s_q"), sem("s_kv"), sem("s_eqT"), sem("s_ctx")
        s_num, s_attnT, s_wo = sem("s_num"), sem("s_attnT"), sem("s_wo")
        s_x2T, s_lg = sem("s_x2T"), sem("s_lg")
        s_qmax, s_qsub, s_mask, s_den, s_attn = sem("s_qmax"), sem("s_qsub"), sem("s_mask"), sem("s_den"), sem("s_attn")
        s_res, s_st, s_mv, s_x2, s_lgo = sem("s_res"), sem("s_st"), sem("s_mv"), sem("s_x2"), sem("s_lgo")
        s_expk, s_vc, s_expq, s_qTe = sem("s_expk"), sem("s_vc"), sem("s_expq"), sem("s_qTe")
        s_aTe, s_x2Te, s_xh, s_x2h, s_wh = sem("s_aTe"), sem("s_x2Te"), sem("s_xh"), sem("s_x2h"), sem("s_wh")
        s_wl, s_ve, s_rstd, s_x2l, s_xl, s_x2b = (
            sem("s_wl"), sem("s_ve"), sem("s_rstd"), sem("s_x2l"), sem("s_xl"), sem("s_x2b"))
        s_r, s_rexp, s_rsub, s_hot, s_rank, s_ranked, s_slots, s_experts = (
            sem("s_r"), sem("s_rexp"), sem("s_rsub"), sem("s_hot"), sem("s_rank"), sem("s_ranked"),
            sem("s_slots"), sem("s_experts"))
        ld_rows, ld_b2, ld_res, st_y = sems("ld_rows", 2), sems("ld_b2", 2), sems("ld_res", 2), sems("st_y", 2)
        ld_sc, st_sc = sems("ld_sc", 4), sems("st_sc", 4)
        ld_acc, ld_g, st_out = sems("ld_acc", 2 * GROUP), sems("ld_g", 2 * GROUP), sems("st_out", 2 * GROUP)
        s_T, s_h, s_y = sem("s_T"), sem("s_h"), sem("s_y")
        s_XT, s_g, s_hh = sem("s_XT"), sem("s_g"), sem("s_hh")
        s_lo, s_yo = sem("s_lo"), sem("s_yo")
        s_idx, s_cadd, s_cst, s_cmv = sem("s_idx"), sem("s_cadd"), sem("s_cst"), sem("s_cmv")
        s_cfin, s_cve, s_crstd = sem("s_cfin"), sem("s_cve"), sem("s_crstd")

        def sums(c):
            return acc[c % (2 * GROUP)] if c < IN_YO else yo[(SLOT_TILES + c // 2) % 2][:, c % 2, :]

        def normalised_at(c):
            first_ = c // GROUP * GROUP - GROUP
            return [first_ + q for q in ((), (0,), (1,), (2, 3))[c % GROUP]] if 0 <= first_ < TILES else []

        block = ctx.enter_context(nc.Block())

        def wait(eng, semaphore, n, alone=False):
            if not isinstance(n, int) or n > 0:
                eng.wait_ge(semaphore, n)
            if not isinstance(n, int) and (alone or eng.engine == mybir.EngineType.Pool):
                eng.sem_inc(s_passed, 1)

        def live(t, lag, n=TILES):
            return not isinstance(t, int) or 0 <= t - lag < n

        @contextmanager
        def loop(eng, start, end, by):
            with eng.Fori(0, (end - start) // by) as n:
                yield n * by + start

        def steps_A(eng, step):
            for t in range(BT - 1):
                step(t, t)
            with loop(eng, BT - 1, TILES - 1, BT) as t0:
                for j in range(BT):
                    step(t0 + j, (BT - 1 + j) % BT)
            for t in range(TILES - 1, TILES + A_LAG):
                step(t, t % BT)

        def half_of(k):
            return (k // 2) % 2

        def loads(t, k, per, more):
            return (t - k) * (16 // per) + (k // per + more) * 16

        def one(view, i):
            return view[i] if isinstance(i, int) else view[bass.ds(i, 1)].rearrange("a p n -> p (a n)")

        def w_part(t, part):
            return W[:, part * ALL_W + t * CHUNK:part * ALL_W + (t + 1) * CHUNK] if isinstance(t, int) else \
                W[:, bass.ds(t * CHUNK + part * ALL_W, CHUNK)]

        tok_v = tok_d.rearrange("(t p) n -> t p n", p=P)
        res_v = res_d.rearrange("(t p) n -> t p n", p=P)
        x_v = x_d.rearrange("(t p) n -> t p n", p=P)
        out_v = out_d.rearrange("(t p) n -> t p n", p=P)
        yt_v = ytok_d.rearrange("(t p) n -> t p n", p=P)

        def ffn_tiles(eng, tile, first, before_slots=lambda: None):
            first(tile)
            with loop(eng, 3, HEAD, 2) as i0:
                for j in range(2):
                    tile(i0 + j, (3 + j) % 2, None)
            if HEAD % 2 == 0:
                tile(HEAD - 1, 1, None)
            before_slots()
            with loop(eng, HEAD, TAIL - 1, 2) as i0:
                for j in range(2):
                    tile(i0 + j, (HEAD + j) % 2, i0 + (j - HEAD))
            tile(TAIL - 1, (TAIL - 1) % 2, SLOT_TILES - 1)

        def tail_tiles(eng, tile):
            pairs = (N_FFN - 1 - TAIL) // 2
            for i in range(TAIL, N_FFN - 1 - 2 * pairs):
                tile(i, i % 2, True)
            with loop(eng, N_FFN - 1 - 2 * pairs, N_FFN - 1, 2) as i0:
                for j in range(2):
                    tile(i0 + j, (N_FFN - 1 + j) % 2, True)
            tile(N_FFN - 1, (N_FFN - 1) % 2, False)

        @block.sync
        def _(sp):
            sp.dma_start(wqkv_f, wqkv_d).then_inc(s_wq, 16)
            sp.dma_start(xT[0], xT_d[:, :, 0:TILE]).then_inc(ld_xT[0], 16)
            sp.dma_start(const[:], const_d).then_inc(s_const, 16)
            sp.dma_start(b2s[:], b2_d[EXPERTS:EXPERTS + 1, :].rearrange("a n -> (a n)").partition_broadcast(P))\
                .then_inc(ld_b2s, 16)
            sp.dma_start(wout, wout_d).then_inc(s_w0, 16)
            sp.dma_start(rw[:], rw_d).then_inc(s_w0, 16)
            sp.dma_start(b1[:], b1_d).then_inc(s_w0, 16)
            sp.dma_start(stage[0], ffn_d[0]).then_inc(ld_w[0], 16)
            zero_v = slot_d.rearrange("s n -> (s n)").rearrange("(t p m) -> t p m", t=TILES, p=P)

            def step(t, k):
                if live(t, 0):
                    wait(sp, s_res, t - 3)
                    sp.dma_start(xr[k % 4], one(x_v, t)).then_inc(ld_xr[k % 4], 16)
                if k % 2 == 0 and live(t, -2) and (isinstance(t, int) or k < BT - 2):
                    wait(sp, s_xl, t)
                    src = xT_d[:, :, (t + 2) * P:(t + 4) * P] if isinstance(t, int) else \
                        xT_d[:, :, bass.ds((t + 2) * P, TILE)]
                    sp.dma_start(xT[half_of(k + 2)], src).then_inc(ld_xT[half_of(k + 2)], 16)
                if not isinstance(t, int) and k == BT - 2:
                    wait(sp, s_xl, t, alone=True)
                    sp.dma_start(xT[0], xT_d[:, :, bass.ds((t + 2) * P, TILE)]).then_inc(ld_xT[0], 16)
                if live(t, 4):
                    wait(sp, s_x2l, t - 3)
                    sp.dma_start(one(tok_v, t - 4), x2s[k % 2]).then_inc(st_rows[k % 2], 16)
                    wait(sp, s_x2b, t - 3)
                    sp.dma_start(one(res_v, t - 4), x2b[k % 2]).then_inc(st_res[k % 2], 16)
                if live(t, 0):
                    if isinstance(t, int) and t == 0:
                        sp.wait_ge(s_init, 3)
                    sp.dma_start(one(zero_v, t), zero[:]).then_inc(st_zero, 16)
                if live(t, -1):
                    wait(sp, s_wl, t)
                    sp.dma_start(stage[(k + 1) % 2], one(ffn_d, t + 1)).then_inc(ld_w[(k + 1) % 2], 16)

            def tiles_of(view):
                return view.rearrange("(t h p) n -> t p h n", h=2, p=P)

            ffn_tok, ffn_slot, res_t = tiles_of(tok_d), tiles_of(slot_d), tiles_of(res_d)
            sc_v = tok_d.rearrange("(g t p) n -> g p t n", t=GROUP, p=P)
            y_tok, y_slot = tiles_of(ytok_d), tiles_of(yslot_d)

            def of(view, i):
                return view[i] if isinstance(i, int) else view[bass.ds(i, 1)].rearrange("a p h n -> p (a h) n")

            def load_rows(i, p, view, j):
                wait(sp, s_T, 2 * (i - 1))
                sp.dma_start(rows[p], of(view, j)).then_inc(ld_rows[p], 16)

            for t in range(BT):
                step(t, t)
            with loop(sp, BT, TILES - BT, BT) as t0:
                for k in range(BT):
                    step(t0 + k, k)
            for t in range(TILES - BT, TILES + A_LAG):
                if t == TILES + 1:
                    sp.wait_ge(s_xl, TILES)
                    for i in range(2):
                        sp.wait_ge(st_rows[i], 16 * 2)
                    for i in range(2):
                        load_rows(i, i, ffn_tok, i)
                step(t, t % BT)

            sp.wait_ge(s_lgo, TILES)
            for i in range(2):
                sp.wait_ge(st_res[i], 16 * TILES // 2)
                sp.wait_ge(st_rows[i], 16 * TILES // 2)

            def load_addend(i, p, n, j):
                if n is None:
                    sp.dma_start(res[j % 2], res_t[j]).then_inc(ld_res[j % 2], 16)
                else:
                    e = sp.value_load(expert_i[0:1, n:n + 1] if isinstance(n, int) else expert_i[0:1, bass.ds(n, 1)],
                                      min_val=0, max_val=EXPERTS - 1)
                    b = (p - HEAD) % 2
                    sp.dma_start(b2[b], b2_d[bass.ds(e, 1), :].rearrange("a n -> (a n)").partition_broadcast(P))\
                        .then_inc(ld_b2[b], 16)

            def store_y(i, p, view, j):
                wait(sp, s_yo, 2 * (i + 1))
                sp.dma_start(of(view, j), yo[p]).then_inc(st_y[p], 16)

            for i in range(2):
                load_addend(i, i, None, i)

            def load_sc(g):
                wait(sp, st_sc[g % 4], 16 * TOP * GROUP * (g // 4))
                sp.dma_start(sc[g % 4], sc_v[g]).then_inc(ld_sc[g % 4], 16)

            def head(i, p):
                load_rows(i + 2, p, ffn_tok, i + 2)
                store_y(i, p, y_tok, i)
                load_addend(i + 2, p, None, i + 2)

            load_sc(0)
            load_sc(1)
            for i in range(HEAD - 2):
                if i == 1:
                    sp.wait_ge(s_slots, 1)
                    load_sc(2)
                    load_sc(3)
                if i >= HEAD - 2 - GROUPS // 2:
                    load_sc(i + GROUPS - HEAD + 2)
                head(i, i % 2)

            def load_acc(c):
                i = c // 2 + (SLOT_TILES if c // 2 >= HEAD else 0)
                wait(sp, st_y[i % 2], 16 * (i // 2 + 1))
                wait(sp, st_out[c % (2 * GROUP)], 16 * (c // (2 * GROUP)))
                sp.dma_start(acc[c % (2 * GROUP)], yt_v[c]).then_inc(ld_acc[c % (2 * GROUP)], 16)

            for q in range(4):
                sp.wait_ge(st_sc[q], 16 * TOP * TILES // 4)
            for i in range(HEAD - 2, HEAD):
                p = i % 2
                load_rows(i + 2, p, ffn_slot, i + 2 - HEAD)
                store_y(i, p, y_tok, i)
                if i == HEAD - 2:
                    sp.wait_ge(s_experts, 1)
                load_addend(i + 2, p, i + 2 - HEAD, None)
            with loop(sp, HEAD, TAIL - 3, 2) as i0:
                for j in range(2):
                    p = (HEAD + j) % 2
                    i = i0 + j
                    n = i0 + (j - HEAD)
                    load_rows(i + 2, p, ffn_slot, n + 2)
                    store_y(i, p, y_slot, n)
                    load_addend(i + 2, p, n + 2, None)
            for c in range(2 * GROUP):
                load_acc(c)
            for i in range(TAIL - 3, TAIL):
                p = i % 2
                if i + 2 < TAIL:
                    load_rows(i + 2, p, ffn_slot, i + 2 - HEAD)
                else:
                    load_rows(i + 2, p, ffn_tok, i + 2 - SLOT_TILES)
                store_y(i, p, y_slot, i - HEAD)
                load_addend(i + 2, p, i + 2 - HEAD if i + 2 < TAIL else None, i + 2 - SLOT_TILES)

            def store_out(c):
                wait(sp, s_cfin, c + 1)
                sp.dma_start(out_v[c], sums(c)).then_inc(st_out[c % (2 * GROUP)], 16)

            def tail(n):
                i = TAIL + n
                if i + 2 < N_FFN:
                    load_rows(i + 2, i % 2, ffn_tok, i + 2 - SLOT_TILES)
                for q in range(GROUP):
                    c = GROUP * n - OFFSET + q
                    if q == GROUP - 1:
                        if i < N_FFN - 2:
                            store_y(i, i % 2, y_tok, i - SLOT_TILES)
                        if i + 2 < N_FFN:
                            load_addend(i + 2, i % 2, None, i + 2 - SLOT_TILES)
                    for o in normalised_at(c - 1):
                        if o + 2 * GROUP < IN_YO:
                            load_acc(o + 2 * GROUP)
                    for o in normalised_at(c):
                        store_out(o)

            for n in range(GROUPS + 2):
                tail(n)
            for q in range(2 * GROUP):
                sp.wait_ge(st_out[q], 16 * TILES // (2 * GROUP))
            sp.wait_ge(st_y[0], 16 * ((N_FFN - 1) // 2))
            sp.wait_ge(st_y[1], 16 * ((N_FFN - 2) // 2))
            sp.wait_ge(st_zero, 16 * TILES)

        @block.tensor
        def _(pe):
            terms = [(0, 0), (0, 1), (1, 0)]

            def context(u, k, r):
                n = 2 * u + r
                wait(pe, s_mask, n + 1)
                if r == 0:
                    wait(pe, s_expk, u + 1)
                    wait(pe, s_vc, u + 1)
                rows_ = slice(BUCKET * r, BUCKET * (r + 1))
                for g in range(KC):
                    mm = pe.matmul(ctx_ps[:, g, :], ek[k % 2][rows_, g * P:(g + 1) * P], vx[k % 2][rows_, g, :],
                                   start=(k == 0 and r == 0 and g == 0), stop=(k == BT - 1 and r == 1),
                                   skip_group_check=True)
                mm.then_inc(s_ctx, 1)

            def project(out, k, lo, hi):
                for n, (xp, wp) in enumerate(terms):
                    for c in range(KC):
                        mm = pe.matmul(out, xs[k % 2][:, xp * KC + c, :], wqkv[wp][:, c, lo:hi],
                                       start=(n == 0 and c == 0), stop=(n == len(terms) - 1 and c == KC - 1))
                return mm

            def turn_x2(t, k):
                if live(t, 4):
                    wait(pe, s_x2, t - 3)
                    wait(pe, s_lgo, t - 4)
                    for g in range(KC):
                        mm = pe.transpose(X2B[:, g * P:(g + 1) * P], x2[k % 2][:, g * P:(g + 1) * P], ident)
                    mm.then_inc(s_x2T, 1)

            def step(t, k):
                if live(t, 1):
                    context(t - 1, (k - 1) % BT, 0)
                    wait(pe, s_expq, t)
                    wait(pe, s_qTe, t - 1)
                    for g in range(KC):
                        mm = pe.transpose(EQT[:, g * P:(g + 1) * P], eq[(k - 1) % 2][:, g * P:(g + 1) * P], ident)
                    mm.then_inc(s_eqT, 1)
                if live(t, 2):
                    wait(pe, s_attn, t - 1)
                    wait(pe, s_aTe, t - 2)
                    for g in range(KC):
                        mm = pe.transpose(ATT[:, g * P:(g + 1) * P], attn[k % 2][:, g * P:(g + 1) * P], ident)
                    mm.then_inc(s_attnT, 1)
                if live(t, 5):
                    wait(pe, s_x2Te, t - 4)
                    for g in range(KC):
                        mm = pe.matmul(X2B[:, D:D + EXPERTS], x2T[:, g * P:(g + 1) * P], rw[:, g, :],
                                       start=(g == 0), stop=(g == KC - 1))
                    mm.then_inc(s_lg, 1)
                if live(t, 0):
                    wait(pe, s_xl, t + 1)
                    wait(pe, s_qsub, t)
                    project(Q[:, 0:D], k, 0, D).then_inc(s_q, 1)
                    wait(pe, s_vc, t)
                    if isinstance(t, int) and t == 0:
                        pe.wait_ge(s_init, 2)
                    project(KV[:, :], k, D, 3 * D).then_inc(s_kv, 1)
                    turn_x2(t, k)
                if live(t, 1):
                    wait(pe, s_qTe, t)
                    wait(pe, s_attn, t - 1)
                    for r in range(2):
                        wait(pe, s_mask, 2 * (t - 1) + r + 1)
                        for g in range(KC):
                            o = g * P + BUCKET * r
                            mm = pe.matmul(num_ps[BUCKET * r:BUCKET * (r + 1), g, :],
                                           qT[(k - 1) % 2][:, o:o + BUCKET], mc[r][:, g, :], start=True, stop=True)
                    mm.then_inc(s_num, 1)
                    context(t - 1, (k - 1) % BT, 1)
                if live(t, 2):
                    if isinstance(t, int) and t == 2:
                        pe.wait_ge(s_w0, 48)
                    wait(pe, s_aTe, t - 1)
                    wait(pe, s_res, t - 2)
                    for g in range(KC):
                        mm = pe.matmul(WO[:, 0:D], attnT[k % 2][:, g * P:(g + 1) * P], wout[:, g, :],
                                       start=(g == 0), stop=(g == KC - 1))
                    mm.then_inc(s_wo, 1)
                if not live(t, 0):
                    turn_x2(t, k)

            pe.wait_ge(s_const, 16)
            pe.wait_ge(s_init, 1)
            steps_A(pe, step)

            def turn(i, p):
                wait(pe, s_XT, 2 * i)
                wait(pe, ld_rows[p], 8 * (i - p) + 16)
                for h in range(2):
                    for k in range(4):
                        mm = pe.transpose(TB[h][:, k * P:(k + 1) * P], rows[p][:, h, k * P:(k + 1) * P], ident_h[:])
                    mm.then_inc(s_T, 1)

            def tile(i, p, n, more=True, ranks=False):
                if n is None:
                    base = EXPERTS * EW
                else:
                    e = pe.value_load(expert_i[0:1, n:n + 1] if isinstance(n, int) else expert_i[0:1, bass.ds(n, 1)],
                                      min_val=0, max_val=EXPERTS - 1)
                    base = pe.snap(e * EW)

                def weights(o, width):
                    return W[:, base + o:base + o + width] if n is None else W[:, bass.ds(base + o, width)]

                wait(pe, s_XT, 2 * i + 2)
                for f in range(FC):
                    wait(pe, s_g, 8 * i + f - 3)
                    for m, (part, xpart) in enumerate(terms):
                        for c in range(KC):
                            mm = pe.matmul(H[f % 4][:, 0:TILE], weights(part * ALL_W + c * FF + f * P, P),
                                           XT[p][:, xpart * KC + c].rearrange("p h n -> p (h n)"),
                                           start=(m == 0 and c == 0), stop=(m == len(terms) - 1 and c == KC - 1))
                    mm.then_inc(s_h, 1)
                    if ranks and f == FC // 2:
                        pe.wait_ge(s_hot, 1)
                        pe.matmul(PRE[:, 0:n_te], const[:, C_TRI:C_TRI + P], r_tmp[0], start=True, stop=True)
                        pe.matmul(TOT[:, 0:n_te], const[:, C_ONE:C_ONE + P], r_tmp[0], start=True, stop=True)\
                            .then_inc(s_rank, 1)
                wait(pe, s_yo, 2 * i)
                late = isinstance(i, int) and i == HEAD - 1
                if more and not late:
                    turn(i + 1, 1 - p)
                if ranks:
                    pe.wait_ge(s_ranked, 1)
                for f in range(FC):
                    if f % 2 == 0:
                        wait(pe, s_lo, 4 * i + f // 2 + 1)
                    for part, src in ((0, hh), (1, hh), (0, hl)):
                        w2 = weights(part * ALL_W + KC * FF + f * D, D)
                        for h in range(2):
                            mm = pe.matmul(Y[h][:, 0:D], src[:, f, h * P:(h + 1) * P], w2,
                                           start=(f == 0 and part == 0 and src is hh),
                                           stop=(f == FC - 1 and src is hl))
                mm.then_inc(s_y, 1)
                if late:
                    turn(i + 1, 1 - p)

            def first(tile):
                pe.wait_ge(s_lgo, TILES)
                turn(0, 0)
                pe.wait_ge(s_wl, W_CHUNKS)
                tile(0, 0, None, ranks=True)
                tile(1, 1, None)
                tile(2, 0, None)

            ffn_tiles(pe, tile, first, lambda: pe.wait_ge(s_experts, 1))
            tail_tiles(pe, lambda i, p, more: tile(i, p, None, more))

        @block.scalar
        def _(act):
            def split_x(t, k):
                wait(act, ld_xT[half_of(k)], loads(t, k, 4, 1))
                wait(act, s_kv, t - 1)
                act.activation(xs[k % 2][:, 0:KC, :], xT[half_of(k)][:, :, (k % 2) * P:(k % 2 + 1) * P], ACT.Copy)\
                    .then_inc(s_xh, 1)

            def take_x2T(t):
                if live(t, 4):
                    wait(act, s_x2T, t - 3)
                    wait(act, s_lg, t - 4)
                    act.activation(x2T, X2B[:, 0:D], ACT.Copy).then_inc(s_x2Te, 1)

            def step(t, k):
                if live(t, 1):
                    wait(act, s_eqT, t)
                    wait(act, s_num, t - 2)
                    act.activation(qT[(k - 1) % 2], EQT[:, 0:D], ACT.Copy).then_inc(s_qTe, 1)
                if live(t, 2):
                    wait(act, s_attnT, t - 1)
                    wait(act, s_wo, t - 3)
                    act.activation(attnT[k % 2], ATT[:, 0:D], ACT.Copy).then_inc(s_aTe, 1)
                if live(t, -1):
                    split_x(t + 1, (k + 1) % BT if isinstance(t, int) else k + 1)
                if live(t, 0):
                    wait(act, s_qsub, t + 1)
                    wait(act, s_eqT, t - 1)
                    act.activation(eq[k % 2], qs, ACT.Exp).then_inc(s_expq, 1)
                if not live(t, 0):
                    take_x2T(t)
                if live(t, 3):
                    wait(act, s_x2, t - 2)
                    wait(act, st_rows[(k + 1) % 2], loads(t, k, 2, -2 + k % 2))
                    act.activation(x2s[(k + 1) % 2][:, 0:D], x2[(k + 1) % 2], ACT.Copy).then_inc(s_x2h, 1)
                if live(t, 0):
                    wait(act, s_kv, t + 1)
                    wait(act, s_ctx, 2 * (t - 1))
                    act.activation(ek[k % 2], KV[:, 0:D], ACT.Exp).then_inc(s_expk, 1)
                    act.activation(vx[k % 2][:, :, 0:P], KV[:, D:2 * D].rearrange("p (g n) -> p g n", g=KC),
                                   ACT.Copy).then_inc(s_vc, 1)
                if live(t, 0):
                    take_x2T(t)
                    wait(act, ld_w[k % 2], loads(t, k, 2, 1))
                    act.activation(w_part(t, 0), stage[k % 2], ACT.Copy).then_inc(s_wh, 1)

            split_x(0, 0)
            act.wait_ge(s_wq, 16)
            act.activation(wqkv[0][:, :, D:3 * D], wqkv_f[:, :, D:3 * D], ACT.Copy).then_inc(s_wqh, 1)
            steps_A(act, step)

            act.wait_ge(s_rsub, 1)
            act.activation(r_tmp[1], r_tmp[0], ACT.Exp).then_inc(s_rexp, 1)

            def evacuate(i, p):
                for h in range(2):
                    wait(act, s_T, 2 * i + h + 1)
                    act.activation(XT[p][:, :, h, :], TB[h].rearrange("p (k n) -> p k n", k=4), ACT.Copy)\
                        .then_inc(s_XT, 1)

            def high(i, g):
                wait(act, s_g, 8 * i + 2 * g + 2)
                if g == 0:
                    wait(act, s_y, i)
                act.activation(hh[:, 2 * g:2 * g + 2].rearrange("p f n -> p (f n)"), hf[g % 2], ACT.Copy)\
                    .then_inc(s_hh, 1)

            def tile(i, p, n, more=True):
                if n is not None:
                    e = act.value_load(expert_i[0:1, n:n + 1] if isinstance(n, int) else expert_i[0:1, bass.ds(n, 1)],
                                       min_val=0, max_val=EXPERTS - 1)
                for f in range(FC):
                    wait(act, s_h, 8 * i + f + 1)
                    if f % 2 == 0:
                        wait(act, s_lo, 4 * i + f // 2 - 1)
                    bias = b1[:, EXPERTS * FC + f:EXPERTS * FC + f + 1] if n is None else b1[:, bass.ds(e * FC + f, 1)]
                    act.activation(hf[f // 2 % 2][:, f % 2 * TILE:(f % 2 + 1) * TILE], H[f % 4][:, 0:TILE],
                                   ACT.Gelu_apprx_tanh, bias=bias).then_inc(s_g, 1)
                    if f % 2 == 0 and f:
                        high(i, f // 2 - 1)
                high(i, FC // 2 - 1)
                if more:
                    evacuate(i + 1, 1 - p)

            def first(tile):
                act.wait_ge(s_lgo, TILES)
                act.wait_ge(s_wl, W_CHUNKS)
                evacuate(0, 0)
                tile(0, 0, None)
                tile(1, 1, None)
                tile(2, 0, None)

            ffn_tiles(act, tile, first, lambda: act.wait_ge(s_experts, 1))
            tail_tiles(act, lambda i, p, more: tile(i, p, None, more))

        @block.vector
        def _(dve):
            def context_before(k, r):
                if k == 0 and r == 0:
                    dve.memset(mc[0][:, :, 0:CW], 0.0).then_inc(s_mask, 1)
                else:
                    dve.tensor_tensor(mc[r][:, :, 0:CW], ctx_ps, mask.unsqueeze(1).to_broadcast([P, KC, CW]),
                                      ALU.mult).then_inc(s_mask, 1)

            def heads(ap):
                return ap.rearrange("p (h d) -> p h d", d=HD)

            def by_chunk(ap):
                return ap.rearrange("p (g h) -> p g h", g=KC)

            def step(t, k):
                if live(t, 1):
                    wait(dve, s_ctx, 2 * (t - 1) + 1)
                    wait(dve, s_num, t - 1)
                    context_before((k - 1) % BT, 1)
                if live(t, 3):
                    wait(dve, s_mv, t - 2)
                    dve.tensor_scalar(ve[(k + 1) % 2], mv[(k + 1) % 2][:, 1:2], EPS, None, ALU.add).then_inc(s_ve, 1)
                if live(t, 0):
                    wait(dve, s_q, t + 1)
                    dve.tensor_reduce(qmax, heads(Q[:, 0:D]), X, ALU.max).then_inc(s_qmax, 1)
                    wait(dve, s_qmax, t + 1)
                    wait(dve, s_expq, t)
                    dve.tensor_tensor(heads(qs), heads(Q[:, 0:D]), qmax.unsqueeze(2).to_broadcast([P, HEADS, HD]),
                                      ALU.subtract).then_inc(s_qsub, 1)
                if live(t, 5):
                    wait(dve, s_lg, t - 4)
                    row = logits[:, t - 5, :] if isinstance(t, int) else \
                        logits[:, bass.ds(t - 5, 1), :].rearrange("p a e -> p (a e)")
                    dve.tensor_tensor(row, X2B[:, D:D + EXPERTS], const[:, C_RB:C_RB + EXPERTS], ALU.add)\
                        .then_inc(s_lgo, 1)
                if live(t, 3):
                    o = (k + 1) % 2
                    wait(dve, s_rstd, t - 2)
                    wait(dve, s_x2l, t - 4)
                    wait(dve, s_x2b, t - 4)
                    wait(dve, s_x2T, t - 4)
                    dve.tensor_scalar(x2[o], s[o], mv[o][:, 0:1], rstd[o], ALU.subtract, ALU.mult).then_inc(s_x2, 1)
                if live(t, 1):
                    wait(dve, s_num, t)
                    dve.tensor_copy(by_chunk(rden), num_ps[:, :, CW:NW]).then_inc(s_den, 1)
                    wait(dve, s_den, 3 * (t - 1) + 1)
                    dve.tensor_tensor(by_chunk(den), num_ps[:, :, P:CW], by_chunk(rden), ALU.max).then_inc(s_den, 1)
                    wait(dve, s_den, 3 * (t - 1) + 2)
                    dve.reciprocal(rden, den).then_inc(s_den, 1)
                if live(t, 0):
                    wait(dve, s_ctx, 2 * t)
                    wait(dve, s_num, t)
                    context_before(k, 0)
                if live(t, 1):
                    wait(dve, s_den, 3 * (t - 1) + 3)
                    wait(dve, s_attnT, t - 2)
                    dve.tensor_tensor(attn[(k - 1) % 2].rearrange("p (g h d) -> p g h d", g=KC, d=HD),
                                      num_ps[:, :, 0:P].rearrange("p g (h d) -> p g h d", d=HD),
                                      by_chunk(rden).unsqueeze(3).to_broadcast([P, KC, GH, HD]), ALU.mult)\
                        .then_inc(s_attn, 1)
                if live(t, 2):
                    wait(dve, s_wo, t - 1)
                    wait(dve, ld_xr[(k - 2) % 4], loads(t, k, 4, 1 if k % 4 >= 2 else 0))
                    dve.tensor_tensor(s[k % 2], WO[:, 0:D], xr[(k - 2) % 4], ALU.add).then_inc(s_res, 1)
                    wait(dve, s_res, t - 1)
                    dve.bn_stats(stats, s[k % 2]).then_inc(s_st, 1)
                    wait(dve, s_rstd, t - 3)
                    wait(dve, s_st, t - 1, alone=True)
                    dve.bn_aggr(mv[k % 2], stats).then_inc(s_mv, 1)

            for j in range(2):
                dve.memset(vx[j][:, :, P:CW], 1.0)
            dve.wait_ge(s_wq, 16)
            dve.tensor_copy(wqkv[0][:, :, 0:D], wqkv_f[:, :, 0:D]).then_inc(s_r, 1)
            dve.wait_ge(s_r, 1)
            dve.tensor_tensor(wqkv[1][:, :, 0:D], wqkv_f[:, :, 0:D], wqkv[0][:, :, 0:D], ALU.subtract).then_inc(s_init, 1)
            dve.wait_ge(s_wqh, 1)
            dve.tensor_tensor(wqkv[1][:, :, D:3 * D], wqkv_f[:, :, D:3 * D], wqkv[0][:, :, D:3 * D], ALU.subtract)\
                .then_inc(s_init, 1)
            dve.wait_ge(s_const, 16)
            for j in range(2):
                for g in range(KC):
                    dve.tensor_scalar(mc[j][:, g, CW:NW], mask[:, P:CW], GUARD, None, ALU.mult)
            dve.tensor_copy(ident_h[:], ident)
            dve.memset(zero[:], 0.0).then_inc(s_init, 1)
            steps_A(dve, step)

            done = [1]

            def then(ins):
                done[0] += 1
                ins.then_inc(s_r, 1)
                dve.wait_ge(s_r, done[0])

            def te(ap):
                return ap.rearrange("p (t e) -> p t e", e=EXPERTS)

            def et(ap):
                return ap.rearrange("p (e t) -> p e t", t=TILES)

            def over_e(ap):
                return ap.unsqueeze(2).to_broadcast([P, TILES, EXPERTS])

            col = [small[:, i * TILES:(i + 1) * TILES] for i in range(8)]
            top1, top2, first_, inv, summed = col[0:5]
            rev = const[:, C_REV:C_REV + EXPERTS].unsqueeze(1).to_broadcast([P, TILES, EXPERTS])
            prob, hot1, hot2, tmp = r_tmp[1], r_tmp[2], r_tmp[3], r_tmp[4]

            def router_softmax():
                dve.wait_ge(s_rexp, 1)
                then(dve.tensor_reduce(summed, te(prob), X, ALU.add))
                then(dve.reciprocal(inv, summed))
                then(dve.tensor_tensor(te(prob), te(prob), over_e(inv), ALU.mult))

            def pick(top, hot):
                then(dve.tensor_reduce(top, te(prob), X, ALU.max))
                then(dve.tensor_tensor(te(tmp), te(prob), over_e(top), ALU.is_equal))
                then(dve.tensor_tensor(te(tmp), te(tmp), rev, ALU.mult))
                then(dve.tensor_reduce(first_, te(tmp), X, ALU.max))
                then(dve.tensor_tensor(te(hot), rev, over_e(first_), ALU.is_equal))

            def pick_first():
                pick(top1, hot1)
                then(dve.scalar_tensor_tensor(prob, hot1, -2.0, prob, ALU.mult, ALU.add))

            def pick_second():
                pick(top2, hot2)
                dve.tensor_tensor(r_tmp[0], hot1, hot2, ALU.add).then_inc(s_hot, 1)

            def gates():
                then(dve.tensor_tensor(summed, top1, top2, ALU.add))
                then(dve.reciprocal(inv, summed))
                then(dve.tensor_tensor(gate[:, 0, :], top1, inv, ALU.mult))
                then(dve.tensor_tensor(gate[:, 1, :], top2, inv, ALU.mult))

            tot, upto, excl = r_tmp[5], r_tmp[6], r_tmp[7]

            def ranks():
                dve.wait_ge(s_rank, 1)
                then(dve.tensor_copy(et(tot), TOT[:, 0:n_te].rearrange("p (t e) -> p e t", e=EXPERTS)))
                dve.tensor_copy(tmp, PRE[:, 0:n_te]).then_inc(s_ranked, 1)

            n_e, end_e, base_e = col[5][:, 0:EXPERTS], col[6][:, 0:EXPERTS], col[7][:, 0:EXPERTS]

            def count():
                then(dve.tensor_tensor_scan(upto, const[:, C_SEG:C_SEG + n_te], tot, 0.0, ALU.mult, ALU.add))
                then(dve.tensor_tensor(excl, upto, tot, ALU.subtract))
                nthr = TILES // 2
                over = tot[:, 0:EXPERTS * nthr].rearrange("p (e j) -> p e j", j=nthr)
                then(dve.tensor_tensor(over, et(upto)[:, :, TILES - 1].unsqueeze(2).to_broadcast([P, EXPERTS, nthr]),
                                       const[:, C_THR:C_THR + nthr].unsqueeze(1).to_broadcast([P, EXPERTS, nthr]),
                                       ALU.is_gt))
                then(dve.tensor_reduce(n_e, over, X, ALU.add))

            def place():
                then(dve.tensor_tensor_scan(end_e, const[:, C_ONE:C_ONE + EXPERTS], n_e, 0.0, ALU.mult, ALU.add))
                then(dve.tensor_tensor(base_e, end_e, n_e, ALU.subtract))
                then(dve.tensor_scalar(base_e, base_e, float(TILE), None, ALU.mult))
                then(dve.tensor_tensor(et(excl), et(excl), base_e.unsqueeze(2).to_broadcast([P, EXPERTS, TILES]),
                                       ALU.add))
                dve.wait_ge(s_ranked, 1)
                then(dve.tensor_tensor(te(tmp), te(tmp), excl.rearrange("p (e t) -> p t e", t=TILES), ALU.add))
                for j, hot in enumerate((hot1, hot2)):
                    then(dve.tensor_tensor(hot, hot, tmp, ALU.mult))
                    then(dve.tensor_reduce(slot_f[:, :, j], te(hot), X, ALU.add))
                dve.tensor_copy(slot_i[:].rearrange("p t j -> p (t j)"), slot_f[:].rearrange("p t j -> p (t j)"))\
                    .then_inc(s_slots, 1)

            def experts():
                for lo in range(0, SLOT_TILES, TILES):
                    n = min(TILES, SLOT_TILES - lo)
                    a = te(small[:, 8 * TILES:8 * TILES + n_te])[:, 0:n, :]
                    then(dve.tensor_tensor(a, end_e.unsqueeze(1).to_broadcast([P, n, EXPERTS]),
                                           const[:, C_J + lo:C_J + lo + n].unsqueeze(2)
                                           .to_broadcast([P, n, EXPERTS]), ALU.is_le))
                    then(dve.tensor_reduce(expert_f[:, lo:lo + n], a, X, ALU.add))
                then(dve.tensor_scalar(expert_f[:], expert_f[:], float(EXPERTS - 1), None, ALU.min))
                dve.tensor_copy(expert_i[:], expert_f[:]).then_inc(s_experts, 1)

            def low(i, g):
                wait(dve, s_hh, 4 * i + g + 1)
                dve.tensor_tensor(hl[:, 2 * g:2 * g + 2].rearrange("p f n -> p (f n)"), hf[g % 2],
                                  hh[:, 2 * g:2 * g + 2].rearrange("p f n -> p (f n)"), ALU.subtract)\
                    .then_inc(s_lo, 1)

            def outputs(i, p, n, a):
                wait(dve, s_y, i + 1)
                wait(dve, st_y[p], 8 * (i - p))
                if n is None:
                    wait(dve, ld_res[a[0]], a[1])
                    for h in range(2):
                        dve.tensor_tensor(yo[p][:, h, :], Y[h][:, 0:D], res[a[0]][:, h, :], ALU.add).then_inc(s_yo, 1)
                else:
                    b = (p - HEAD) % 2
                    wait(dve, ld_b2[b], 8 * (n - b) + 16)
                    for h in range(2):
                        dve.tensor_tensor(yo[p][:, h, :], Y[h][:, 0:D], b2[b], ALU.add).then_inc(s_yo, 1)

            def combine(c):
                b = c % (2 * GROUP)
                if live(c, 0):
                    if c < IN_YO:
                        wait(dve, ld_acc[b], 16 * (c // (2 * GROUP) + 1))
                    else:
                        wait(dve, s_yo, 2 * (c // 2 + SLOT_TILES + 1))
                    wait(dve, ld_g[b], 32 * (c // (2 * GROUP) + 1))
                    dve.scalar_tensor_tensor(sums(c), g1[b], gate[:, 0, c:c + 1], sums(c), ALU.mult, ALU.add)\
                        .then_inc(s_cadd, 1)
                if live(c, 1):
                    wait(dve, s_cadd, 2 * c)
                    wait(dve, s_cmv, c - 1)
                    dve.bn_stats(cstats, sums(c - 1)).then_inc(s_cst, 1)
                if live(c, 0):
                    wait(dve, s_cadd, 2 * c + 1)
                    dve.scalar_tensor_tensor(sums(c), g2[b], gate[:, 1, c:c + 1], sums(c), ALU.mult, ALU.add)\
                        .then_inc(s_cadd, 1)
                if live(c, 1):
                    wait(dve, s_cst, c)
                    dve.bn_aggr(cmv[:, (c - 1) % (2 * GROUP), :], cstats).then_inc(s_cmv, 1)
                    if c % GROUP == 0:
                        j = (c - 1) // GROUP % 2
                        wait(dve, s_cmv, c)
                        dve.tensor_scalar(cve[j], cmv[:, GROUP * j:GROUP * (j + 1), 1], EPS, None, ALU.add)\
                            .then_inc(s_cve, 1)
                for o in normalised_at(c):
                    wait(dve, s_crstd, o // GROUP + 1)
                    dve.tensor_scalar(sums(o), sums(o), cmv[:, o % (2 * GROUP), 0:1],
                                      crstd[o // GROUP % 2][:, o % GROUP:o % GROUP + 1],
                                      ALU.subtract, ALU.mult).then_inc(s_cfin, 1)

            def tile(i, p, n, c0=None, between={}):
                for g in range(4):
                    low(i, g)
                    for q in ((), (0,), (), (1, 2))[g] if c0 is not None else ():
                        combine(c0 + q)
                    for part in between.get(g, ()):
                        part()
                if c0 is None:
                    outputs(i, p, n, (p, 8 * (i - p) + 16))
                else:
                    j = i - SLOT_TILES
                    outputs(i, p, None, (j % 2, 16 * (j // 2 + 1)))
                    combine(c0 + GROUP - 1)

            def first(tile):
                dve.wait_ge(s_lgo, TILES)
                then(dve.tensor_reduce(top1, logits[:], X, ALU.max))
                dve.tensor_tensor(te(r_tmp[0]), logits[:], over_e(top1), ALU.subtract).then_inc(s_rsub, 1)
                router_softmax()
                pick_first()
                pick_second()
                tile(0, 0, None, between={1: (ranks,), 2: (count,), 3: (place,)})
                tile(1, 1, None, between={3: (experts,)})
                tile(2, 0, None)

            ffn_tiles(dve, tile, first)
            gates()
            for i in range(TAIL, N_FFN):
                tile(i, i % 2, None, GROUP * (i - TAIL) - OFFSET)
            for c in range(GROUP * (N_FFN - TAIL) - OFFSET, TILES + GROUP):
                combine(c)

        @block.gpsimd
        def _(pool):
            neg = const[:, C_NEG:C_NEG + 1]

            def split_x(t, k):
                wait(pool, s_xh, t + 1)
                pool.tensor_tensor(xs[k % 2][:, KC:2 * KC, :], xT[half_of(k)][:, :, (k % 2) * P:(k % 2 + 1) * P],
                                   xs[k % 2][:, 0:KC, :], ALU.subtract).then_inc(s_xl, 1)

            def low_weights(t, k):
                wait(pool, s_wh, t + 1)
                pool.tensor_tensor(w_part(t, 1), stage[k % 2], w_part(t, 0), ALU.subtract).then_inc(s_wl, 1)

            def step(t, k):
                if live(t, 3):
                    wait(pool, s_ve, t - 2)
                    wait(pool, s_x2, t - 4)
                    pool.tensor_tensor(rstd[(k + 1) % 2], ve[(k + 1) % 2], neg, ALU.pow).then_inc(s_rstd, 1)
                if live(t, -1):
                    split_x(t + 1, (k + 1) % BT if isinstance(t, int) else k + 1)
                if live(t, 1):
                    low_weights(t - 1, k - 1)
                if live(t, 3):
                    o = (k + 1) % 2
                    wait(pool, s_x2h, t - 2)
                    pool.tensor_tensor(x2s[o][:, D:2 * D], x2[o], x2s[o][:, 0:D], ALU.subtract).then_inc(s_x2l, 1)
                    wait(pool, st_res[o], loads(t, k, 2, -2 + k % 2))
                    pool.tensor_tensor(x2b[o], x2[o], b2s[:], ALU.add).then_inc(s_x2b, 1)

            split_x(0, 0)
            pool.wait_ge(s_const, 16)
            pool.wait_ge(ld_b2s, 16)
            steps_A(pool, step)

            def copy_index(n, g, j):
                src = slot_i[:, GROUP * g:GROUP * (g + 1), :] if isinstance(g, int) else \
                    slot_i[:, bass.ds(g * GROUP, GROUP), :]
                pool.tensor_copy(idx[j], src.rearrange("p t j -> p (t j)")).then_inc(s_idx, 1)
                wait(pool, s_idx, n)

            def scatter(g, j):
                wait(pool, ld_sc[j], 4 * (g - j) + 16)
                copy_index(g + 1, g, j)
                for t in range(GROUP):
                    for k in range(TOP):
                        pool.indirect_dma_start(slot_d, bass.IndirectOffsetOnAxis(ap=idx[j][:, TOP * t + k:TOP * t + k + 1], axis=0),
                                                sc[j][:, t, :], None).then_inc(st_sc[j], 16)

            pool.wait_ge(s_slots, 1)
            pool.wait_ge(st_zero, 16 * TILES)
            with loop(pool, 0, GROUPS, 4) as g0:
                for j in range(4):
                    scatter(g0 + j, j)

            for p in range(2):
                pool.wait_ge(st_y[p], 16 * ((TAIL + 1 - p) // 2))
            for q in range(4):
                pool.wait_ge(st_sc[q], 16 * TOP * TILES // 4)

            def gather(m, j):
                copy_index(GROUPS + 1 + m, m, j)
                for q in range(GROUP):
                    c = m * GROUP + q
                    b = j * GROUP + q
                    wait(pool, s_cadd, 2 * (c - 2 * GROUP + 1))
                    for k, g in enumerate((g1, g2)):
                        pool.indirect_dma_start(g[b], None, yslot_d,
                                                bass.IndirectOffsetOnAxis(ap=idx[j][:, TOP * q + k:TOP * q + k + 1], axis=0))\
                            .then_inc(ld_g[b], 16)

            def inverse_deviation(m, j):
                wait(pool, s_cve, m + 1)
                pool.tensor_tensor(crstd[j], cve[j], neg.to_broadcast([P, GROUP]), ALU.pow).then_inc(s_crstd, 1)

            gather(0, 0)
            gather(1, 1)
            inverse_deviation(0, 0)
            with loop(pool, 2, GROUPS, 2) as m0:
                for j in range(2):
                    gather(m0 + j, j)
                    inverse_deviation(m0 + (j - 1), 1 - j)
            inverse_deviation(GROUPS - 1, 1)


def kernel(**inputs):
    import numpy as np
    import concourse.bacc as bacc
    from concourse.bass_utils import run_bass_kernel_spmd

    a = {k: np.asarray(v) for k, v in inputs.items()}

    def chunks(m):
        return np.ascontiguousarray(m.reshape(-1, P, m.shape[1]).transpose(1, 0, 2))

    x = a["L0_attn_x"].reshape(N_TOK, D)
    w1 = np.concatenate([a["L0_ffn_spec_w1"], a["L0_ffn_shared_w1"][None]])
    w2 = np.concatenate([a["L0_ffn_spec_w2"], a["L0_ffn_shared_w2"][None]])
    b1 = np.concatenate([a["L0_ffn_spec_b1"], a["L0_ffn_shared_b1"][None]])
    b2 = np.concatenate([a["L0_ffn_spec_b2"], a["L0_ffn_shared_b2"][None]])
    ffn = np.concatenate([chunks(m.T).reshape(P, -1) for uv in zip(w1, w2) for m in uv], 1)\
        .reshape(P, W_CHUNKS, CHUNK).transpose(1, 0, 2)
    p, n = np.arange(P), np.arange(EXPERTS * TILES)
    const = np.zeros((P, C_N), np.float32)
    const[:, C_ID:C_ID + P] = np.eye(P)
    const[:, C_MASK:C_MASK + P] = p[:, None] // HD == p[None] // HD
    const[:, C_MASK + P:C_MASK + CW] = p[:, None] // HD == np.arange(GH)[None]
    const[:, C_TRI:C_TRI + P] = p[:, None] < p[None]
    const[:, C_ONE:C_ONE + P] = 1
    const[:, C_REV:C_REV + EXPERTS] = EXPERTS - np.arange(EXPERTS)
    const[:, C_SEG:C_SEG + len(n)] = n % TILES != 0
    const[:, C_THR:C_THR + TILES // 2] = TILE * np.arange(TILES // 2)
    const[:, C_J:C_J + SLOT_TILES] = np.arange(SLOT_TILES)
    const[:, C_NEG] = NEG
    const[:, C_RB:C_RB + EXPERTS] = a["L0_ffn_router_b"]
    arrays = {
        "xT": chunks(x.T), "x": x, "wqkvT": chunks(a["L0_attn_W_qkv"].T), "woutT": chunks(a["L0_attn_W_out"].T),
        "ffn": ffn, "b1": np.ascontiguousarray(b1.reshape(-1, FC, P).transpose(2, 0, 1).reshape(P, -1)),
        "b2": b2, "rwT": chunks(a["L0_ffn_router_w"].T), "const": const,
    }
    arrays = {k: np.ascontiguousarray(v) for k, v in arrays.items()}
    nc = bacc.Bacc("TRN2", target_bir_lowering=False, num_devices=1)
    args = [nc.dram_tensor(f"in_{k}", v.shape, F32, kind="ExternalInput").ap() for k, v in arrays.items()]
    out = nc.dram_tensor("out", (N_TOK, D), F32, kind="ExternalOutput").ap()
    build(nc, *args, out)
    r = run_bass_kernel_spmd(nc, [{f"in_{k}": v for k, v in arrays.items()}], core_ids=[0])
    return r.results[0]["out"].reshape(B, T, D)
```
